# Optimizing a Trainium2 kernel written in Bass

```python
import numpy as np
import jax
import jax.numpy as jnp

def _softmax(x, axis=-1):
    return jax.nn.softmax(x, axis=axis)

def _gelu(x):
    return jax.nn.gelu(x, approximate=True)

def _silu(x):
    return jax.nn.silu(x)

def _sigmoid(x):
    return jax.nn.sigmoid(x)

def _layernorm(x, axis=-1, eps=1e-05):
    m = jnp.mean(x, axis=axis, keepdims=True)
    v = jnp.var(x, axis=axis, keepdims=True)
    return (x - m) / jnp.sqrt(v + eps)

def _scatter_add(tgt, idx, src, axis=0):
    return tgt.at[idx].add(src)

def _segment_sum(src, seg, n):
    return jax.ops.segment_sum(src, seg, n)
kernel_name = 'mk_gnn_resnorm_d2_gnn_r64_6af5fe'

def setup_inputs(seed: int=0):
    np.random.seed(seed)
    _w = jnp.asarray

    def _rec_inputs():
        import jax
        import jax.numpy as jnp
        _gk = jax.random.key(seed)
        x = -0.0002928 + 1 * jax.random.normal(jax.random.fold_in(_gk, 1), (512, 128), jnp.float32)
        _s = jax.random.randint(jax.random.fold_in(_gk, 2), (8192,), 0, 512, jnp.int32)
        _d = jax.random.randint(jax.random.fold_in(_gk, 3), (8192,), 0, 512, jnp.int32)
        _loop = jnp.arange(512, dtype=jnp.int32)
        src = jnp.concatenate([_s, _d, _loop])
        dst = jnp.concatenate([_d, _s, _loop])
        _o = jnp.argsort(dst, stable=True)
        src = src[_o]
        dst = dst[_o]
        edge_type_3 = jax.random.randint(jax.random.fold_in(_gk, 13), (16896,), 0, 3, jnp.int32)
        edge_weight = jax.random.uniform(jax.random.fold_in(_gk, 14), (16896,), jnp.float32, 0.0, 0.999998)
        return (x, src, dst, edge_type_3, edge_weight)
    x, src, dst, edge_type_3, edge_weight = _rec_inputs()

    def _L0_gnn_setup():
        import jax, jax.numpy as jnp
        import numpy as np
        N = 512
        D = 16
        C = 128
        H = 128

        def _lstm_last(seq, wih, whh, bih, bhh):
            n = seq.shape[1]
            h0 = jnp.zeros((n, wih.shape[0] // 4), seq.dtype)
            b = bih + bhh

            def step(carry, x_t):
                h, c = carry
                g = x_t @ wih.T + h @ whh.T + b
                i, f, gg, o = jnp.split(g, 4, axis=-1)
                c = jax.nn.sigmoid(f) * c + jax.nn.sigmoid(i) * jnp.tanh(gg)
                h = jax.nn.sigmoid(o) * jnp.tanh(c)
                return ((h, c), None)
            (h, _), _ = jax.lax.scan(step, (h0, h0), seq)
            return h

        def _sage_conv(x, src, wih, whh, bih, bhh, wl, bl, wr):
            n, c = x.shape
            d = src.shape[0] // n
            msgs = x[src].reshape(n, d, c)
            aggr = _lstm_last(jnp.swapaxes(msgs, 0, 1), wih, whh, bih, bhh)
            return aggr @ wl.T + bl + x @ wr.T
        key = jax.random.key(seed)
        ks = jax.random.split(key, 20)
        x = jax.random.normal(ks[0], (N, C), dtype=jnp.float32)
        src = jax.random.randint(ks[1], (N * D,), 0, N, dtype=jnp.int32)
        dst = jnp.repeat(jnp.arange(N, dtype=jnp.int32), D)
        edge_index = jnp.stack([src, dst])
        s = 1.0 / np.sqrt(C)

        def mat(k, o, i):
            return jax.random.uniform(k, (o, i), jnp.float32, -s, s)

        def vec(k, o):
            return jax.random.uniform(k, (o,), jnp.float32, -s, s)
        inp = {'x': x, 'edge_index': edge_index}
        for k0, base in [(2, 'conv1'), (10, 'conv2')]:
            inp[f'{base}_wih'] = mat(ks[k0 + 0], 4 * C, C)
            inp[f'{base}_whh'] = mat(ks[k0 + 1], 4 * C, C)
            inp[f'{base}_bih'] = vec(ks[k0 + 2], 4 * C)
            inp[f'{base}_bhh'] = vec(ks[k0 + 3], 4 * C)
            inp[f'{base}_wl'] = mat(ks[k0 + 4], H, C)
            inp[f'{base}_bl'] = vec(ks[k0 + 5], H)
            inp[f'{base}_wr'] = mat(ks[k0 + 6], H, C)
        return inp
    _L0_gnn_all = _L0_gnn_setup()
    _L0_gnn_in = {k: v for k, v in _L0_gnn_all.items() if k in ('conv1_wih', 'conv1_whh', 'conv1_bih', 'conv1_bhh', 'conv1_wl', 'conv1_bl', 'conv1_wr', 'conv2_wih', 'conv2_whh', 'conv2_bih', 'conv2_bhh', 'conv2_wl', 'conv2_bl', 'conv2_wr')}
    del _L0_gnn_all

    def _L1_gnn_setup():
        import jax, jax.numpy as jnp
        import numpy as np
        N_NODES = 50000
        N_EDGES = 12500
        IN_FEATS = 128
        OUT_FEATS = 128
        N_REL = 3
        key = jax.random.key(seed)
        k1, k2, k3, k4, k5, k6 = jax.random.split(key, 6)
        feature = jax.random.normal(k1, (N_NODES, IN_FEATS), dtype=jnp.float32)
        bound = float(np.sqrt(6.0 / IN_FEATS))
        weight = jax.random.uniform(k2, (N_REL, IN_FEATS, OUT_FEATS), dtype=jnp.float32, minval=-bound, maxval=bound)
        norm = jax.random.uniform(k3, (N_EDGES,), dtype=jnp.float32)
        src = jax.random.randint(k4, (N_EDGES,), 0, N_NODES)
        dst = jax.random.randint(k5, (N_EDGES,), 0, N_NODES)
        rel_type = jax.random.randint(k6, (N_EDGES,), 0, N_REL)
        return {'feature': feature, 'weight': weight, 'norm': norm, 'src': src, 'dst': dst, 'rel_type': rel_type}
    _L1_gnn_all = _L1_gnn_setup()
    _L1_gnn_in = {k: v for k, v in _L1_gnn_all.items() if k in ('weight',)}
    del _L1_gnn_all
    return {'x': x, 'src': src, 'dst': dst, 'edge_type_3': edge_type_3, 'edge_weight': edge_weight, 'L0_gnn_conv1_wih': _L0_gnn_in['conv1_wih'], 'L0_gnn_conv1_whh': _L0_gnn_in['conv1_whh'], 'L0_gnn_conv1_bih': _L0_gnn_in['conv1_bih'], 'L0_gnn_conv1_bhh': _L0_gnn_in['conv1_bhh'], 'L0_gnn_conv1_wl': _L0_gnn_in['conv1_wl'], 'L0_gnn_conv1_bl': _L0_gnn_in['conv1_bl'], 'L0_gnn_conv1_wr': _L0_gnn_in['conv1_wr'], 'L0_gnn_conv2_wih': _L0_gnn_in['conv2_wih'], 'L0_gnn_conv2_whh': _L0_gnn_in['conv2_whh'], 'L0_gnn_conv2_bih': _L0_gnn_in['conv2_bih'], 'L0_gnn_conv2_bhh': _L0_gnn_in['conv2_bhh'], 'L0_gnn_conv2_wl': _L0_gnn_in['conv2_wl'], 'L0_gnn_conv2_bl': _L0_gnn_in['conv2_bl'], 'L0_gnn_conv2_wr': _L0_gnn_in['conv2_wr'], 'L1_gnn_weight': _L1_gnn_in['weight']}

def reference(x, src, dst, edge_type_3, edge_weight, L0_gnn_conv1_wih, L0_gnn_conv1_whh, L0_gnn_conv1_bih, L0_gnn_conv1_bhh, L0_gnn_conv1_wl, L0_gnn_conv1_bl, L0_gnn_conv1_wr, L0_gnn_conv2_wih, L0_gnn_conv2_whh, L0_gnn_conv2_bih, L0_gnn_conv2_bhh, L0_gnn_conv2_wl, L0_gnn_conv2_bl, L0_gnn_conv2_wr, L1_gnn_weight):
    import jax
    import jax.numpy as jnp

    def _L0_gnn_ref(x, edge_index, conv1_wih, conv1_whh, conv1_bih, conv1_bhh, conv1_wl, conv1_bl, conv1_wr, conv2_wih, conv2_whh, conv2_bih, conv2_bhh, conv2_wl, conv2_bl, conv2_wr):
        import jax, jax.numpy as jnp
        import numpy as np
        N = 512
        D = 16
        C = 128
        H = 128

        def _lstm_last(seq, wih, whh, bih, bhh):
            n = seq.shape[1]
            h0 = jnp.zeros((n, wih.shape[0] // 4), seq.dtype)
            b = bih + bhh

            def step(carry, x_t):
                h, c = carry
                g = x_t @ wih.T + h @ whh.T + b
                i, f, gg, o = jnp.split(g, 4, axis=-1)
                c = jax.nn.sigmoid(f) * c + jax.nn.sigmoid(i) * jnp.tanh(gg)
                h = jax.nn.sigmoid(o) * jnp.tanh(c)
                return ((h, c), None)
            (h, _), _ = jax.lax.scan(step, (h0, h0), seq)
            return h

        def _sage_conv(x, src, wih, whh, bih, bhh, wl, bl, wr):
            n, c = x.shape
            d = src.shape[0] // n
            msgs = x[src].reshape(n, d, c)
            aggr = _lstm_last(jnp.swapaxes(msgs, 0, 1), wih, whh, bih, bhh)
            return aggr @ wl.T + bl + x @ wr.T
        src = edge_index[0]
        h = _sage_conv(x, src, conv1_wih, conv1_whh, conv1_bih, conv1_bhh, conv1_wl, conv1_bl, conv1_wr)
        h = jax.nn.relu(h)
        out = _sage_conv(h, src, conv2_wih, conv2_whh, conv2_bih, conv2_bhh, conv2_wl, conv2_bl, conv2_wr)
        return out

    def _L1_gnn_ref(feature, weight, norm, src, dst, rel_type):
        import jax, jax.numpy as jnp
        import numpy as np
        N_NODES = 50000
        N_EDGES = 12500
        IN_FEATS = 128
        OUT_FEATS = 128
        N_REL = 3
        hr = jnp.einsum('ni,rio->rno', feature, weight)
        msg = hr[rel_type, src] * norm[:, None]
        h = jax.ops.segment_sum(msg, dst, num_segments=feature.shape[0])
        return jax.nn.relu(h)
    edge_index = jnp.stack([src, dst])
    x = _layernorm(x + _L0_gnn_ref(x, edge_index, L0_gnn_conv1_wih, L0_gnn_conv1_whh, L0_gnn_conv1_bih, L0_gnn_conv1_bhh, L0_gnn_conv1_wl, L0_gnn_conv1_bl, L0_gnn_conv1_wr, L0_gnn_conv2_wih, L0_gnn_conv2_whh, L0_gnn_conv2_bih, L0_gnn_conv2_bhh, L0_gnn_conv2_wl, L0_gnn_conv2_bl, L0_gnn_conv2_wr), axis=-1)
    x = _layernorm(x + _L1_gnn_ref(x, L1_gnn_weight, edge_weight, src, dst, edge_type_3), axis=-1)
    return x

_drawn_inputs = setup_inputs


def setup_inputs(seed=0):
    import zlib

    import numpy as np

    out = dict(_drawn_inputs(seed))
    spreads = {}
    factors = {'L0_gnn_conv1_whh': 7.393, 'L0_gnn_conv1_bih': 4.515, 'L0_gnn_conv1_bhh': 4.999}
    for name, (base, spread) in spreads.items():
        noise = np.random.default_rng([zlib.crc32(name.encode()), seed]).standard_normal(out[name].shape)
        drawn = base * np.exp(spread * noise) if base else spread * noise
        out[name] = jnp.asarray(drawn.astype(out[name].dtype))
    for name, factor in factors.items():
        out[name] = (out[name] * factor).astype(out[name].dtype)
    return out
```

```python
from contextlib import ExitStack

import numpy as np

import concourse.bass as bass
from concourse import mybir

F32 = mybir.dt.float32
F16 = mybir.dt.float16
I32 = mybir.dt.int32
ACT = mybir.ActivationFunctionType
ALU = mybir.AluOpType

P = 128
H_SCALE = 2.0 ** 8
W_SCALE = 2.0 ** 7
G_SCALE = H_SCALE * W_SCALE
EPS = 1e-5

GATE_I, GATE_F, GATE_G, GATE_O = range(4)
BANKS = ((GATE_G, GATE_I), (GATE_F, GATE_O))


def build_program(nc, x, src, dst, rel, edge_w, wih, whh, bih, bhh, wl, bl, wr, rgcn_w, out):
    N, C = x.shape
    E = src.shape[0]
    T = E // N
    NR = rgcn_w.shape[0]
    K = N // P
    G = 4 * C
    HN = N // 2
    UN = 3
    IT = T // UN
    SLOTS = UN * K
    TILES = E // P
    ET = TILES // SLOTS
    assert C == P and T % UN == 0 and TILES % SLOTS == 0 and N == 512

    gate_table = [nc.dram_tensor(f"gate_table{l}", (N, 2 * G), F16, kind="Internal").ap() for l in range(2)]
    msg_table = nc.dram_tensor("msg_table", (N, NR * C), F32, kind="Internal").ap()
    msg_rows = msg_table.rearrange("n (r c) -> (n r) c", c=C)

    with ExitStack() as ctx:
        def sb(name, shape, dt):
            return ctx.enter_context(nc.sbuf_tensor(name, shape, dt))

        def sem(name):
            return ctx.enter_context(nc.semaphore(name))

        def pair(name):
            return [sem(f"{name}_{h}") for h in range(2)]

        gates = ctx.enter_context(nc.psum_tensor("gates", [P, 2, 2, 2 * HN], F32))
        work = ctx.enter_context(nc.psum_tensor("work", [P, 4, 512], F32))
        gate_bank = [gates[:, b // 2, b % 2, :] for b in range(4)]

        x_nodes = sb("x_nodes", [P, K, C], F32)
        wih_rows = [sb(f"wih_rows{l}", [P, 4, C], F32) for l in range(2)]
        whh_rows = [sb(f"whh_rows{l}", [P, 4, C], F32) for l in range(2)]
        lin_rows = sb("lin_rows", [P, 4, C], F32)
        bias_in = sb("bias_in", [1, 2, 2, G], F32)
        bias_sum = sb("bias_sum", [1, 2, G], F32)
        bl1_col = sb("bl1_col", [P, 1], F32)
        bl2_row = sb("bl2_row", [1, C], F32)
        rgcn_sb = sb("rgcn_sb", [P, NR, C], F32)
        src_by_node = sb("src_by_node", [P, K, T], I32)
        src_steps = sb("src_steps", [P, T, K], I32)
        src_edges = sb("src_edges", [P, TILES], I32)
        dst_edges = sb("dst_edges", [P, TILES], I32)
        rel_edges = sb("rel_edges", [P, TILES], I32)
        norm_edges = sb("norm_edges", [P, TILES], F32)
        dst_f = sb("dst_f", [P, TILES], F32)
        msg_index = sb("msg_index", [P, TILES], I32)
        index_now = sb("index_now", [P, SLOTS], I32)

        ident = sb("ident", [P, P], F32)
        ident_scaled = sb("ident_scaled", [P, P], F16)
        ones_row = sb("ones_row", [1, P], F32)
        zeros16 = sb("zeros16", [P, 512], F16)
        node_iota_i = sb("node_iota_i", [P, N], I32)
        node_iota = sb("node_iota", [P, N], F16)

        xT = sb("xT", [P, N], F32)
        wihT = [sb(f"wihT{l}", [P, G], F32) for l in range(2)]
        whh_hi = [sb(f"whh_hi{l}", [P, G], F16) for l in range(2)]
        whh_lo = [sb(f"whh_lo{l}", [P, G], F16) for l in range(2)]
        linT = sb("linT", [P, 4, C], F32)

        table_sb = sb("table_sb", [P, K, 2, G], F16)
        rows = sb("rows", [P, SLOTS, 2, G], F16)

        act_g = sb("act_g", [P, 2, HN], F32)
        act_i = sb("act_i", [P, 2, HN], F32)
        act_f = sb("act_f", [P, 2, HN], F32)
        act_o = sb("act_o", [P, 2, HN], F32)
        tanh_c = sb("tanh_c", [P, 2, HN], F32)
        prod_ig = sb("prod_ig", [P, 2, HN], F32)
        prod_fc = sb("prod_fc", [P, 2, HN], F32)
        cell = sb("cell", [P, 2, HN], F32)
        h_full = sb("h_full", [P, 2, HN], F32)
        h_hi = sb("h_hi", [P, 2, HN], F16)
        h_lo = sb("h_lo", [P, 2, HN], F16)
        h_last = sb("h_last", [P, N], F32)
        h1T = sb("h1T", [P, N], F32)

        y = sb("y", [P, K, C], F32)
        stats = sb("stats", [P, K, 6], F32)
        mean_var = sb("mean_var", [P, K, 2], F32)
        var_eps = sb("var_eps", [P, K], F32)
        std = sb("std", [P, K], F32)
        rstd = sb("rstd", [P, K], F32)
        x2 = sb("x2", [P, K, C], F32)
        x2T = sb("x2T", [P, N], F32)
        table2_sb = sb("table2_sb", [P, K, NR * C], F32)
        edge_rows = sb("edge_rows", [P, SLOTS, C], F32)
        msg_hi = sb("msg_hi", [P, SLOTS, C], F16)
        msg_lo = sb("msg_lo", [P, SLOTS, C], F16)
        dst_onehot = sb("dst_onehot", [P, SLOTS, N], F16)
        aggT = sb("aggT", [P, N], F32)
        result = sb("result", [P, K, C], F32)

        x_loaded = sem("x_loaded")
        wih_loaded = [sem(f"wih_loaded{l}") for l in range(2)]
        whh_loaded = [sem(f"whh_loaded{l}") for l in range(2)]
        bias_loaded = sem("bias_loaded")
        src_loaded = sem("src_loaded")
        lin_loaded = sem("lin_loaded")
        bl_loaded = sem("bl_loaded")
        rgcn_loaded = sem("rgcn_loaded")
        edges_loaded = sem("edges_loaded")
        ident_ready = sem("ident_ready")
        ident16_ready = sem("ident16_ready")
        iota_ready = sem("iota_ready")
        index_ready = sem("index_ready")
        edge_ready = sem("edge_ready")
        bias_ready = sem("bias_ready")
        turned = sem("turned")
        turned_act = sem("turned_act")
        turned_dve = sem("turned_dve")
        whh_ready = sem("whh_ready")
        projected = sem("projected")
        table_hi = sem("table_hi")
        table_lo = sem("table_lo")
        table_stored = sem("table_stored")
        rows_in = [sem(f"rows_in{s}") for s in range(SLOTS)]
        rows_free = pair("rows_free")
        index_staged = sem("index_staged")
        held = sem("held")
        gates0 = pair("gates0")
        gates1 = pair("gates1")
        gi_ready = pair("gi_ready")
        f_ready = pair("f_ready")
        o_ready = pair("o_ready")
        ig_ready = pair("ig_ready")
        fc_ready = pair("fc_ready")
        c_ready = pair("c_ready")
        tanh_ready = pair("tanh_ready")
        h_hi_ready = pair("h_hi_ready")
        h_full_ready = pair("h_full_ready")
        h_lo_ready = pair("h_lo_ready")
        h_last_ready = sem("h_last_ready")
        sage_done = sem("sage_done")
        h1T_ready = sem("h1T_ready")
        ln = sem("ln")
        ln_std = sem("ln_std")
        x2_ready = sem("x2_ready")
        x2_turned = sem("x2_turned")
        x2T_ready = sem("x2T_ready")
        msg_projected = sem("msg_projected")
        msg_taken = sem("msg_taken")
        msg_stored = sem("msg_stored")
        msg_free = sem("msg_free")
        msg_hi_ready = sem("msg_hi_ready")
        msg_lo_ready = sem("msg_lo_ready")
        onehot_ready = sem("onehot_ready")
        agg_done = sem("agg_done")
        aggT_ready = sem("aggT_ready")
        agg_turned = sem("agg_turned")
        result_ready = sem("result_ready")
        result_stored = sem("result_stored")

        block = ctx.enter_context(nc.Block())

        @block.sync
        def _(sp):
            sp.dma_start(x_nodes[:, :, :], x.rearrange("(k p) c -> p k c", p=P)).then_inc(x_loaded, 16)
            sp.dma_start(wih_rows[0][:, :, :], wih[0].rearrange("(g p) c -> p g c", p=P)).then_inc(wih_loaded[0], 16)
            for l in range(2):
                sp.dma_start(bias_in[:, l, 0, :], bih[l].rearrange("(a g) -> a g", a=1)).then_inc(bias_loaded, 16)
                sp.dma_start(bias_in[:, l, 1, :], bhh[l].rearrange("(a g) -> a g", a=1)).then_inc(bias_loaded, 16)
            sp.dma_start(whh_rows[0][:, :, :], whh[0].rearrange("(g p) c -> p g c", p=P)).then_inc(whh_loaded[0], 16)
            sp.dma_start(src_by_node[:, :, :], src.rearrange("(k p t) -> p k t", p=P, k=K)).then_inc(src_loaded, 16)
            sp.dma_start(wih_rows[1][:, :, :], wih[1].rearrange("(g p) c -> p g c", p=P)).then_inc(wih_loaded[1], 16)
            sp.dma_start(whh_rows[1][:, :, :], whh[1].rearrange("(g p) c -> p g c", p=P)).then_inc(whh_loaded[1], 16)
            for l in range(2):
                sp.dma_start(lin_rows[:, 2 * l, :], wl[l]).then_inc(lin_loaded, 16)
                sp.dma_start(lin_rows[:, 2 * l + 1, :], wr[l]).then_inc(lin_loaded, 16)
            sp.dma_start(bl1_col[:, :], bl[0].rearrange("(p a) -> p a", a=1)).then_inc(bl_loaded, 16)
            sp.dma_start(bl2_row[:, :], bl[1].rearrange("(a c) -> a c", a=1)).then_inc(bl_loaded, 16)
            for k in range(K):
                sp.wait_ge(table_lo, k + 1)
                sp.dma_start(gate_table[0][k * P:(k + 1) * P, :],
                             table_sb[:, k, :, :].rearrange("p a g -> p (a g)")).then_inc(table_stored, 16)
            sp.dma_start(rgcn_sb[:, :, :], rgcn_w.rearrange("r i o -> i r o")).then_inc(rgcn_loaded, 16)
            for buf, a in ((src_edges, src), (dst_edges, dst), (rel_edges, rel), (norm_edges, edge_w)):
                sp.dma_start(buf[:, :], a.rearrange("(p t) -> p t", p=P)).then_inc(edges_loaded, 16)
            for k in range(K):
                sp.wait_ge(table_lo, K + k + 1)
                sp.dma_start(gate_table[1][k * P:(k + 1) * P, :],
                             table_sb[:, k, :, :].rearrange("p a g -> p (a g)")).then_inc(table_stored, 16)
            for k in range(K):
                sp.wait_ge(msg_taken, k + 1)
                sp.dma_start(msg_table[k * P:(k + 1) * P, :], table2_sb[:, k, :]).then_inc(msg_stored, 16)
            for k in range(K):
                sp.wait_ge(result_ready, k + 1)
                sp.dma_start(out[k * P:(k + 1) * P, :], result[:, k, :]).then_inc(result_stored, 16)
            sp.wait_ge(result_stored, 16 * K)

        @block.gpsimd
        def _(pool):
            def hold(semaphore, value):
                pool.wait_ge(semaphore, value)
                pool.sem_inc(held, 1)

            def stage(j, indices, staged):
                pool.tensor_copy(index_now[:, j * K:(j + 1) * K], indices).then_inc(index_staged, 1)
                hold(index_staged, staged)

            pool.memset(ident[:, :], 0.0).then_inc(ident_ready, 1)
            pool.wait_ge(ident_ready, 1)
            pool.affine_select(out=ident[:, :], in_=ident[:, :], compare_op=ALU.not_equal, fill=1.0, base=0,
                               pattern=[[-1, P]], channel_multiplier=1).then_inc(ident_ready, 1)
            pool.iota(node_iota_i[:, :], pattern=[[1, N]], base=0, channel_multiplier=0).then_inc(iota_ready, 1)
            for h in range(2):
                pool.sem_inc(rows_free[h], UN)
            pool.sem_inc(msg_lo_ready, SLOTS)
            pool.wait_ge(index_ready, 1)

            for l in range(2):
                pool.wait_ge(table_stored, 16 * K * (l + 1))
                with pool.Fori(0, IT) as i:
                    for j in range(UN):
                        for h in range(2):
                            hold(rows_free[h], i * UN + (l * T + j + 1))
                        stage(j, src_steps[:, bass.ds(i * UN + j, 1), :].rearrange("p t k -> p (t k)"),
                              i * UN + (l * T + j + 1))
                        for s in range(j * K, (j + 1) * K):
                            pool.indirect_dma_start(
                                rows[:, s, :, :].rearrange("p a g -> p (a g)"), None, gate_table[l],
                                bass.IndirectOffsetOnAxis(index_now[:, s:s + 1], axis=0)).then_inc(rows_in[s], 16)

            pool.wait_ge(edge_ready, 2)
            pool.wait_ge(msg_stored, 16 * K)
            with pool.Fori(0, ET) as i:
                for j in range(UN):
                    hold(msg_lo_ready, i * SLOTS + (j + 1) * K)
                    stage(j, msg_index[:, bass.ds(i * SLOTS + j * K, K)], i * UN + (2 * T + j + 1))
                    for s in range(j * K, (j + 1) * K):
                        pool.indirect_dma_start(
                            edge_rows[:, s, :], None, msg_rows,
                            bass.IndirectOffsetOnAxis(index_now[:, s:s + 1], axis=0)).then_inc(rows_in[s], 16)

        @block.scalar
        def _(act):
            act.preload_act_table(ACT.Sigmoid)

            def take(group, dest):
                act.wait_ge(turned, group + 1)
                act.activation(dest, work[:, group % 4, :], ACT.Copy).then_inc(turned_act, 1)

            def table_parts(l):
                if l == 1:
                    act.wait_ge(table_stored, 16 * K)
                for k in range(K):
                    act.wait_ge(projected, l * K + k + 1)
                    act.activation(table_sb[:, k, 0, :], gate_bank[k], ACT.Copy).then_inc(table_hi, 1)

            take(0, xT[:, :])
            table_parts(0)
            take(3, wihT[1][:, :])
            take(5, linT[:, :, :].rearrange("p a c -> p (a c)"))

            for l in range(2):
                with act.Fori(0, IT) as i:
                    for j in range(UN):
                        def count(more=0):
                            return i * UN + (l * T + j + 1 + more)
                        for h in range(2):
                            bank = gates[:, h, 0, :]
                            act.wait_ge(gates0[h], count())
                            act.activation(act_g[:, h, :], bank[:, 0:HN], ACT.Tanh, scale=1 / G_SCALE)
                            act.activation(act_i[:, h, :], bank[:, HN:], ACT.Sigmoid,
                                           scale=1 / G_SCALE).then_inc(gi_ready[h], 1)
                            bank = gates[:, h, 1, :]
                            act.wait_ge(gates1[h], count())
                            act.activation(act_f[:, h, :], bank[:, 0:HN], ACT.Sigmoid,
                                           scale=1 / G_SCALE).then_inc(f_ready[h], 1)
                            act.activation(act_o[:, h, :], bank[:, HN:], ACT.Sigmoid,
                                           scale=1 / G_SCALE).then_inc(o_ready[h], 1)
                            act.wait_ge(c_ready[h], count())
                            act.activation(tanh_c[:, h, :], cell[:, h, :], ACT.Tanh).then_inc(tanh_ready[h], 1)
                if l == 0:
                    act.wait_ge(bl_loaded, 32)
                    act.wait_ge(sage_done, 1)
                    act.activation(h1T[:, :], work[:, 2, :], ACT.Relu, bias=bl1_col[:, :]).then_inc(h1T_ready, 1)
                    table_parts(1)

            act.preload_act_table(ACT.Sqrt)

            def norm_std(which):
                act.wait_ge(ln, which * (2 * K + 3) + 2 * K + 2)
                act.activation(std[:, :], var_eps[:, :], ACT.Sqrt).then_inc(ln_std, 1)

            norm_std(0)
            act.wait_ge(x2_turned, 1)
            act.activation(x2T[:, :], work[:, 0, :], ACT.Copy).then_inc(x2T_ready, 1)
            for k in range(0, K, 2):
                act.wait_ge(msg_projected, k + 1)
                if k >= 2:
                    act.wait_ge(msg_taken, k)
                act.activation(table2_sb[:, k, :], gate_bank[k][:, 0:NR * C], ACT.Copy).then_inc(msg_taken, 1)

            with act.Fori(0, ET) as i:
                for s in range(SLOTS):
                    act.wait_ge(rows_in[s], i * 16 + 16 * (2 * IT + 1))
                    act.wait_ge(msg_free, i * SLOTS + (s + 1))
                    act.activation(msg_hi[:, s, :], edge_rows[:, s, :], ACT.Copy,
                                   scale=norm_edges[:, bass.ds(i * SLOTS + s, 1)]).then_inc(msg_hi_ready, 1)

            act.wait_ge(agg_done, 1)
            act.activation(aggT[:, :], work[:, 1, :], ACT.Relu).then_inc(aggT_ready, 1)
            norm_std(1)

        @block.vector
        def _(dve):
            def take(group, dest):
                dve.wait_ge(turned, group + 1)
                dve.tensor_copy(dest, work[:, group % 4, :]).then_inc(turned_dve, 1)

            def split_whh(group, l):
                dve.wait_ge(turned, group + 1)
                dve.tensor_scalar(whh_hi[l][:, :], work[:, group % 4, :], W_SCALE, None,
                                  op0=ALU.mult).then_inc(whh_ready, 1)
                dve.wait_ge(whh_ready, 2 * l + 1)
                dve.scalar_tensor_tensor(whh_lo[l][:, :], work[:, group % 4, :], W_SCALE, whh_hi[l][:, :],
                                         op0=ALU.mult, op1=ALU.subtract).then_inc(whh_ready, 1)

            def table_parts(l):
                for k in range(K):
                    dve.wait_ge(table_hi, l * K + k + 1)
                    dve.tensor_tensor(table_sb[:, k, 1, :], gate_bank[k], table_sb[:, k, 0, :],
                                      ALU.subtract).then_inc(table_lo, 1)

            def zero_state(l):
                for h in range(2):
                    dve.memset(cell[:, h, :], 0.0)
                    dve.memset(h_hi[:, h, :], 0.0).then_inc(h_hi_ready[h], 1)
                    dve.memset(h_lo[:, h, :], 0.0).then_inc(h_lo_ready[h], 1)

            dve.memset(ones_row[:, :], 1.0)
            dve.memset(zeros16[:, :], 0.0)
            dve.wait_ge(bias_loaded, 64)
            dve.tensor_tensor(bias_sum[:, :, :], bias_in[:, :, 0, :], bias_in[:, :, 1, :],
                              ALU.add).then_inc(bias_ready, 1)
            take(1, wihT[0][:, :])
            dve.wait_ge(ident_ready, 2)
            dve.tensor_scalar(ident_scaled[:, :], ident[:, :], G_SCALE, None, op0=ALU.mult).then_inc(ident16_ready, 1)
            dve.wait_ge(src_loaded, 16)
            dve.tensor_copy(src_steps[:, :, :].rearrange("p t k -> p k t"), src_by_node[:, :, :]).then_inc(index_ready, 1)
            split_whh(2, 0)
            zero_state(0)
            table_parts(0)
            split_whh(4, 1)
            dve.wait_ge(iota_ready, 1)
            dve.tensor_copy(node_iota[:, :], node_iota_i[:, :])
            dve.wait_ge(edges_loaded, 64)
            dve.tensor_copy(dst_f[:, :], dst_edges[:, :]).then_inc(edge_ready, 1)
            dve.scalar_tensor_tensor(msg_index[:, :], src_edges[:, :], float(NR), rel_edges[:, :],
                                     op0=ALU.mult, op1=ALU.add).then_inc(edge_ready, 1)

            for l in range(2):
                if l == 1:
                    zero_state(1)
                with dve.Fori(0, IT) as i:
                    for j in range(UN):
                        def count(more=0):
                            return i * UN + (l * T + j + 1 + more)
                        for h in range(2):
                            dve.wait_ge(gi_ready[h], count())
                            dve.tensor_tensor(prod_ig[:, h, :], act_i[:, h, :], act_g[:, h, :],
                                              ALU.mult).then_inc(ig_ready[h], 1)
                            dve.wait_ge(f_ready[h], count())
                            dve.tensor_tensor(prod_fc[:, h, :], act_f[:, h, :], cell[:, h, :],
                                              ALU.mult).then_inc(fc_ready[h], 1)
                            dve.wait_ge(ig_ready[h], count())
                            dve.wait_ge(fc_ready[h], count())
                            dve.tensor_tensor(cell[:, h, :], prod_ig[:, h, :], prod_fc[:, h, :],
                                              ALU.add).then_inc(c_ready[h], 1)
                            dve.wait_ge(o_ready[h], count(1))
                            dve.wait_ge(tanh_ready[h], count())
                            dve.scalar_tensor_tensor(h_hi[:, h, :], act_o[:, h, :], H_SCALE, tanh_c[:, h, :],
                                                     op0=ALU.mult, op1=ALU.mult).then_inc(h_hi_ready[h], 1)
                            dve.scalar_tensor_tensor(h_full[:, h, :], act_o[:, h, :], H_SCALE, tanh_c[:, h, :],
                                                     op0=ALU.mult, op1=ALU.mult).then_inc(h_full_ready[h], 1)
                            dve.wait_ge(h_hi_ready[h], count(l + 1))
                            dve.wait_ge(h_full_ready[h], count())
                            dve.tensor_tensor(h_lo[:, h, :], h_full[:, h, :], h_hi[:, h, :],
                                              ALU.subtract).then_inc(h_lo_ready[h], 1)
                for h in range(2):
                    dve.wait_ge(h_full_ready[h], T * (l + 1))
                dve.tensor_scalar(h_last[:, :], h_full[:, :, :].rearrange("p h n -> p (h n)"), 1 / H_SCALE, None,
                                  op0=ALU.mult).then_inc(h_last_ready, 1)
                if l == 0:
                    table_parts(1)

            steps = [0]

            def link(ins):
                steps[0] += 1
                ins.then_inc(ln, 1)

            def layer_norm(which, summand, residual, dest, ready):
                link(dve.tensor_tensor(y[:, :, :], summand, residual, ALU.add))
                dve.wait_ge(ln, steps[0])
                for k in range(K):
                    link(dve.bn_stats(stats[:, k, :], y[:, k, :]))
                for k in range(K):
                    dve.wait_ge(ln, steps[0] - K + 1)
                    link(dve.bn_aggr(mean_var[:, k, :], stats[:, k, :]))
                dve.wait_ge(ln, steps[0])
                link(dve.tensor_scalar(var_eps[:, :], mean_var[:, :, 1], EPS, None, op0=ALU.add))
                dve.wait_ge(ln_std, which + 1)
                link(dve.reciprocal(rstd[:, :], std[:, :]))
                dve.wait_ge(ln, steps[0])
                for k in range(K):
                    dve.tensor_scalar(dest[:, k, :], y[:, k, :], mean_var[:, k, 0:1], rstd[:, k:k + 1],
                                      op0=ALU.subtract, op1=ALU.mult).then_inc(ready, 1)

            dve.wait_ge(sage_done, 2)
            layer_norm(0, work[:, 3, :].rearrange("p (k c) -> p k c", k=K), x_nodes[:, :, :], x2, x2_ready)
            for k in range(1, K, 2):
                dve.wait_ge(msg_projected, k + 1)
                dve.wait_ge(msg_taken, k)
                dve.tensor_copy(table2_sb[:, k, :], gate_bank[k][:, 0:NR * C]).then_inc(msg_taken, 1)

            with dve.Fori(0, ET) as i:
                for s in range(SLOTS):
                    dve.wait_ge(msg_free, i * SLOTS + (s + 1))
                    dve.tensor_scalar(dst_onehot[:, s, :], node_iota[:, :], dst_f[:, bass.ds(i * SLOTS + s, 1)], None,
                                      op0=ALU.is_equal).then_inc(onehot_ready, 1)
                    dve.wait_ge(msg_hi_ready, i * SLOTS + (s + 1))
                    dve.scalar_tensor_tensor(msg_lo[:, s, :], edge_rows[:, s, :],
                                             norm_edges[:, bass.ds(i * SLOTS + s, 1)], msg_hi[:, s, :],
                                             op0=ALU.mult, op1=ALU.subtract
                                             ).then_inc(msg_lo_ready, 1)

            dve.wait_ge(agg_turned, 1)
            layer_norm(1, work[:, 2, :].rearrange("p (k c) -> p k c", k=K), x2[:, :, :], result, result_ready)

        @block.tensor
        def _(pe):
            def turn(group, blocks):
                for b, a in enumerate(blocks):
                    mm = pe.transpose(work[:, group % 4, b * P:(b + 1) * P], a, ident[:, :])
                mm.then_inc(turned, 1)

            def project(l, inT):
                for k in range(K):
                    pe.matmul(gate_bank[k], inT[:, k * P:(k + 1) * P], wihT[l][:, :], start=True, stop=False)
                    pe.matmul(gate_bank[k], ones_row[:, :], bias_sum[:, l, :],
                              start=False, stop=True).then_inc(projected, 1)

            pe.wait_ge(ident_ready, 2)
            pe.wait_ge(x_loaded, 16)
            turn(0, [x_nodes[:, k, :] for k in range(K)])
            pe.wait_ge(wih_loaded[0], 16)
            turn(1, [wih_rows[0][:, g, :] for g in range(4)])
            pe.wait_ge(whh_loaded[0], 16)
            turn(2, [whh_rows[0][:, g, :] for g in range(4)])
            pe.wait_ge(turned_act, 1)
            pe.wait_ge(turned_dve, 1)
            pe.wait_ge(bias_ready, 1)
            project(0, xT)
            pe.wait_ge(wih_loaded[1], 16)
            turn(3, [wih_rows[1][:, g, :] for g in range(4)])
            pe.wait_ge(whh_loaded[1], 16)
            turn(4, [whh_rows[1][:, g, :] for g in range(4)])
            pe.wait_ge(lin_loaded, 64)
            turn(5, [lin_rows[:, g, :] for g in range(4)])
            for h in range(2):
                pe.sem_inc(o_ready[h], 1)
            pe.wait_ge(ident16_ready, 1)
            pe.wait_ge(whh_ready, 2)
            pe.wait_ge(table_lo, K)

            for l in range(2):
                with pe.Fori(0, IT) as i:
                    for j in range(UN):
                        def count(more=0):
                            return i * UN + (l * T + j + 1 + more)
                        for h in range(2):
                            for k in (2 * h, 2 * h + 1):
                                pe.wait_ge(rows_in[j * K + k], i * 16 + 16 * (l * IT + 1))
                            pe.wait_ge(o_ready[h], count())
                            for b in range(2):
                                for q, gate in enumerate(BANKS[b]):
                                    for k in range(2):
                                        for part in range(2):
                                            mm = pe.matmul(
                                                gates[:, h, b, q * HN + k * P:q * HN + (k + 1) * P],
                                                rows[:, j * K + 2 * h + k, part, gate * P:(gate + 1) * P],
                                                ident_scaled[:, :], start=(q == 0 and k == 0 and part == 0),
                                                stop=False, skip_group_check=True)
                            mm.then_inc(rows_free[h], 1)

                            def products(b, weights, state, last=False):
                                for q, gate in enumerate(BANKS[b]):
                                    for w in weights:
                                        mm = pe.matmul(gates[:, h, b, q * HN:(q + 1) * HN],
                                                       w[:, gate * P:(gate + 1) * P], state[:, h, :],
                                                       start=False, stop=last and q == 1, skip_group_check=True)
                                return mm
                            hi, lo = whh_hi[l], whh_lo[l]
                            pe.wait_ge(h_hi_ready[h], count(l))
                            products(0, (hi, lo), h_hi)
                            products(1, (hi, lo), h_hi)
                            pe.wait_ge(h_lo_ready[h], count(l))
                            products(0, (hi,), h_lo, True).then_inc(gates0[h], 1)
                            products(1, (hi,), h_lo, True).then_inc(gates1[h], 1)
                pe.wait_ge(h_last_ready, l + 1)
                if l == 0:
                    pe.wait_ge(turned_act, 3)
                    pe.matmul(work[:, 2, :], linT[:, 0, :], h_last[:, :], start=True, stop=False)
                    pe.matmul(work[:, 2, :], linT[:, 1, :], xT[:, :], start=False, stop=True).then_inc(sage_done, 1)
                    pe.wait_ge(h1T_ready, 1)
                    project(1, h1T)
                    pe.wait_ge(whh_ready, 4)
                    pe.wait_ge(table_lo, 2 * K)
                else:
                    for k in range(K):
                        o = work[:, 3, k * P:(k + 1) * P]
                        pe.matmul(o, h_last[:, k * P:(k + 1) * P], linT[:, 2, :], start=True, stop=False)
                        pe.matmul(o, h1T[:, k * P:(k + 1) * P], linT[:, 3, :], start=False, stop=False)
                        mm = pe.matmul(o, ones_row[:, :], bl2_row[:, :], start=False, stop=True)
                    mm.then_inc(sage_done, 1)

            for k in range(K):
                pe.wait_ge(x2_ready, k + 1)
                mm = pe.transpose(work[:, 0, k * P:(k + 1) * P], x2[:, k, :], ident[:, :])
            mm.then_inc(x2_turned, 1)
            pe.wait_ge(x2T_ready, 1)
            pe.wait_ge(rgcn_loaded, 16)
            for k in range(K):
                pe.matmul(gate_bank[k][:, 0:NR * C], x2T[:, k * P:(k + 1) * P],
                          rgcn_sb[:, :, :].rearrange("p r c -> p (r c)"), start=True, stop=True).then_inc(msg_projected, 1)

            pe.sem_inc(msg_free, SLOTS)
            pe.matmul(work[:, 1, :], zeros16[:, 0:P], zeros16[:, :], start=True, stop=False, skip_group_check=True)
            with pe.Fori(0, ET) as i:
                for s in range(SLOTS):
                    pe.wait_ge(msg_hi_ready, i * SLOTS + (s + 1))
                    pe.wait_ge(onehot_ready, i * SLOTS + (s + 1))
                    pe.matmul(work[:, 1, :], msg_hi[:, s, :], dst_onehot[:, s, :], start=False, stop=False,
                              skip_group_check=True)
                    pe.wait_ge(msg_lo_ready, i * SLOTS + (SLOTS + s + 1))
                    pe.matmul(work[:, 1, :], msg_lo[:, s, :], dst_onehot[:, s, :], start=False, stop=False,
                              skip_group_check=True).then_inc(msg_free, 1)
            pe.matmul(work[:, 1, :], zeros16[:, 0:P], zeros16[:, :], start=False, stop=True,
                      skip_group_check=True).then_inc(agg_done, 1)
            pe.wait_ge(aggT_ready, 1)
            for k in range(K):
                mm = pe.transpose(work[:, 2, k * P:(k + 1) * P], aggT[:, k * P:(k + 1) * P], ident[:, :])
            mm.then_inc(agg_turned, 1)


_LSTM = ["wih", "whh", "bih", "bhh", "wl", "bl", "wr"]
_INS = (["x", "src", "dst", "edge_type_3", "edge_weight"]
        + [f"L0_gnn_conv{l}_{w}" for l in (1, 2) for w in _LSTM] + ["L1_gnn_weight"])


def kernel(**inputs):
    import concourse.bacc as _bacc
    from concourse.bass_utils import run_bass_kernel_spmd as _run

    nc = _bacc.Bacc("TRN2", target_bir_lowering=False, num_devices=1)
    arrays, aps = {}, {}
    for name in _INS:
        a = np.ascontiguousarray(inputs[name])
        arrays[f"in_{name}"] = a
        aps[name] = nc.dram_tensor(f"in_{name}", a.shape, mybir.dt.from_np(a.dtype), kind="ExternalInput").ap()
    out = nc.dram_tensor("out", inputs["x"].shape, F32, kind="ExternalOutput").ap()
    both = {w: [aps[f"L0_gnn_conv{l}_{w}"] for l in (1, 2)] for w in _LSTM}
    build_program(nc, aps["x"], aps["src"], aps["dst"], aps["edge_type_3"], aps["edge_weight"],
                  both["wih"], both["whh"], both["bih"], both["bhh"], both["wl"], both["bl"], both["wr"],
                  aps["L1_gnn_weight"], out)
    r = _run(nc, [arrays], core_ids=[0])
    return r.results[0]["out"]
```

```python
from contextlib import ExitStack

import numpy as np

import concourse.bass as bass
from concourse import mybir

F32 = mybir.dt.float32
F16 = mybir.dt.float16
I32 = mybir.dt.int32
ACT = mybir.ActivationFunctionType
ALU = mybir.AluOpType

P = 128
H_SCALE = 2.0 ** 8
W_SCALE = 2.0 ** 7
G_SCALE = H_SCALE * W_SCALE
EPS = 1e-5
WARM = 6

GATE_I, GATE_F, GATE_G, GATE_O = range(4)
BANKS = ((GATE_I, GATE_F), (GATE_G, GATE_O))


def build_program(nc, x, src, dst, rel, edge_w, wih, whh, bih, bhh, wl, bl, wr, rgcn_w, out):
    N, C = x.shape
    E = src.shape[0]
    T = E // N
    NR = rgcn_w.shape[0]
    K = N // P
    G = 4 * C
    HN = N // 2
    UN = 3
    IT = T // UN
    SLOTS = UN * K
    TILES = E // P
    ET = TILES // SLOTS
    assert C == P and T % UN == 0 and TILES % SLOTS == 0 and N == 512

    gate_table = [nc.dram_tensor(f"gate_table{l}", (N, 2 * G), F16, kind="Internal").ap() for l in range(2)]
    msg_table = nc.dram_tensor("msg_table", (N, NR * C), F32, kind="Internal").ap()
    msg_rows = msg_table.rearrange("n (r c) -> (n r) c", c=C)

    with ExitStack() as ctx:
        def sb(name, shape, dt):
            return ctx.enter_context(nc.sbuf_tensor(name, shape, dt))

        def sem(name):
            return ctx.enter_context(nc.semaphore(name))

        def pair(name):
            return [sem(f"{name}_{h}") for h in range(2)]

        gates = ctx.enter_context(nc.psum_tensor("gates", [P, 2, 2, 2 * HN], F32))
        work = ctx.enter_context(nc.psum_tensor("work", [P, 4, 512], F32))
        gate_bank = [gates[:, b // 2, b % 2, :] for b in range(4)]
        table_bank = [gate_bank, [work[:, b, :] for b in (0, 1, 3, 2)]]

        x_nodes = sb("x_nodes", [P, K, C], F32)
        wih_rows = [sb(f"wih_rows{l}", [P, 4, C], F32) for l in range(2)]
        whh_rows = [sb(f"whh_rows{l}", [P, 4, C], F32) for l in range(2)]
        lin_rows = sb("lin_rows", [P, 4, C], F32)
        bias_in = sb("bias_in", [1, 2, 2, G], F32)
        bias_sum = sb("bias_sum", [1, 2, G], F32)
        bias_hi = sb("bias_hi", [1, 2, G], F16)
        bias_lo = sb("bias_lo", [1, 2, G], F16)
        bl1_col = sb("bl1_col", [P, 1], F32)
        bl2_row = sb("bl2_row", [1, C], F32)
        rgcn_sb = sb("rgcn_sb", [P, NR, C], F32)
        src_by_node = sb("src_by_node", [P, K, T], I32)
        src_steps = sb("src_steps", [P, T, K], I32)
        src_edges = sb("src_edges", [P, TILES], I32)
        dst_edges = sb("dst_edges", [P, TILES], I32)
        rel_edges = sb("rel_edges", [P, TILES], I32)
        norm_edges = sb("norm_edges", [P, TILES], F32)
        dst_f = sb("dst_f", [P, TILES], F32)
        msg_index = sb("msg_index", [P, TILES], I32)
        index_now = sb("index_now", [P, SLOTS], I32)

        ident = sb("ident", [P, P], F32)
        ident_scaled = sb("ident_scaled", [P, P], F16)
        ones_row = sb("ones_row", [1, P], F32)
        ones16 = sb("ones16", [1, P], F16)
        zeros16 = sb("zeros16", [P, 512], F16)
        node_iota_i = sb("node_iota_i", [P, N], I32)
        node_iota = sb("node_iota", [P, N], F16)

        xT = sb("xT", [P, N], F32)
        wihT = [sb(f"wihT{l}", [P, G], F32) for l in range(2)]
        whh_hi = [sb(f"whh_hi{l}", [P, G], F16) for l in range(2)]
        whh_lo = [sb(f"whh_lo{l}", [P, G], F16) for l in range(2)]
        linT = sb("linT", [P, 4, C], F32)

        table_sb = sb("table_sb", [P, K, 2, G], F16)
        rows = sb("rows", [P, SLOTS, 2, G], F16)

        act_g = sb("act_g", [P, 2, HN], F32)
        act_if = sb("act_if", [P, 2, 2 * HN], F32)
        act_o = sb("act_o", [P, 2, HN], F32)
        tanh_c = sb("tanh_c", [P, 2, HN], F32)
        prod_ig = sb("prod_ig", [P, 2, HN], F32)
        prod_fc = sb("prod_fc", [P, 2, HN], F32)
        cell = sb("cell", [P, 2, HN], F32)
        h_full = sb("h_full", [P, 2, HN], F32)
        h_hi = sb("h_hi", [P, 2, HN], F16)
        h_lo = sb("h_lo", [P, 2, HN], F16)
        h1T = sb("h1T", [P, N], F32)

        y = sb("y", [P, K, C], F32)
        stats = sb("stats", [P, K, 6], F32)
        mean_var = sb("mean_var", [P, K, 2], F32)
        var_eps = sb("var_eps", [P, K], F32)
        std = sb("std", [P, K], F32)
        rstd = sb("rstd", [P, K], F32)
        x2 = sb("x2", [P, K, C], F32)
        x2T = sb("x2T", [P, N], F32)
        table2_sb = sb("table2_sb", [P, K, NR * C], F32)
        edge_rows = sb("edge_rows", [P, SLOTS, C], F32)
        msg_hi = sb("msg_hi", [P, SLOTS, C], F16)
        msg_lo = sb("msg_lo", [P, SLOTS, C], F16)
        dst_onehot = sb("dst_onehot", [P, SLOTS, N], F16)
        aggT = sb("aggT", [P, N], F32)
        result = sb("result", [P, K, C], F32)

        x_loaded = sem("x_loaded")
        wih_loaded = [sem(f"wih_loaded{l}") for l in range(2)]
        whh_loaded = [sem(f"whh_loaded{l}") for l in range(2)]
        bias_loaded = [sem(f"bias_loaded{l}") for l in range(2)]
        src_loaded = sem("src_loaded")
        lin_loaded = sem("lin_loaded")
        bl_loaded = sem("bl_loaded")
        rgcn_loaded = sem("rgcn_loaded")
        edges_loaded = sem("edges_loaded")
        ident_ready = sem("ident_ready")
        ident16_ready = sem("ident16_ready")
        iota_ready = sem("iota_ready")
        index_ready = sem("index_ready")
        edge_ready = sem("edge_ready")
        bias_ready = sem("bias_ready")
        turned = sem("turned")
        turned_act = sem("turned_act")
        turned_dve = sem("turned_dve")
        whh_ready = sem("whh_ready")
        lin_ready = sem("lin_ready")
        warm_ready = sem("warm_ready")
        projected = sem("projected")
        table_hi = sem("table_hi")
        table_lo = sem("table_lo")
        table_stored = sem("table_stored")
        rows_in = [sem(f"rows_in{s}") for s in range(SLOTS)]
        rows_free = pair("rows_free")
        index_staged = sem("index_staged")
        held = sem("held")
        gates0 = pair("gates0")
        gates1 = pair("gates1")
        if_ready = pair("if_ready")
        g_ready = pair("g_ready")
        o_ready = pair("o_ready")
        ig_ready = pair("ig_ready")
        fc_ready = pair("fc_ready")
        c_ready = pair("c_ready")
        tanh_ready = pair("tanh_ready")
        h_hi_ready = pair("h_hi_ready")
        h_full_ready = pair("h_full_ready")
        h_lo_ready = pair("h_lo_ready")
        sage_done = sem("sage_done")
        h1T_ready = sem("h1T_ready")
        ln = sem("ln")
        ln_std = sem("ln_std")
        x2_ready = sem("x2_ready")
        x2_turned = sem("x2_turned")
        x2T_ready = sem("x2T_ready")
        msg_projected = sem("msg_projected")
        msg_taken = sem("msg_taken")
        msg_stored = sem("msg_stored")
        msg_free = sem("msg_free")
        msg_hi_ready = sem("msg_hi_ready")
        msg_lo_ready = sem("msg_lo_ready")
        onehot_ready = sem("onehot_ready")
        agg_done = sem("agg_done")
        aggT_ready = sem("aggT_ready")
        agg_turned = sem("agg_turned")
        result_ready = sem("result_ready")
        result_stored = sem("result_stored")

        block = ctx.enter_context(nc.Block())

        @block.sync
        def _(sp):
            sp.dma_start(x_nodes[:, :, :], x.rearrange("(k p) c -> p k c", p=P)).then_inc(x_loaded, 16)
            sp.dma_start(bias_in[:, 0, 0, :], bih[0].rearrange("(a g) -> a g", a=1)).then_inc(bias_loaded[0], 16)
            sp.dma_start(whh_rows[0][:, :, :], whh[0].rearrange("(g p) c -> p g c", p=P)).then_inc(whh_loaded[0], 16)
            sp.dma_start(src_by_node[:, :, :], src.rearrange("(k p t) -> p k t", p=P, k=K)).then_inc(src_loaded, 16)
            sp.dma_start(wih_rows[1][:, :, :], wih[1].rearrange("(g p) c -> p g c", p=P)).then_inc(wih_loaded[1], 16)
            sp.dma_start(whh_rows[1][:, :, :], whh[1].rearrange("(g p) c -> p g c", p=P)).then_inc(whh_loaded[1], 16)
            sp.dma_start(bias_in[:, 1, 0, :], bih[1].rearrange("(a g) -> a g", a=1)).then_inc(bias_loaded[1], 16)
            sp.dma_start(bias_in[:, 1, 1, :], bhh[1].rearrange("(a g) -> a g", a=1)).then_inc(bias_loaded[1], 16)
            for l in range(2):
                sp.dma_start(lin_rows[:, 2 * l, :], wl[l]).then_inc(lin_loaded, 16)
                sp.dma_start(lin_rows[:, 2 * l + 1, :], wr[l]).then_inc(lin_loaded, 16)
            sp.dma_start(bl1_col[:, :], bl[0].rearrange("(p a) -> p a", a=1)).then_inc(bl_loaded, 16)
            sp.dma_start(bl2_row[:, :], bl[1].rearrange("(a c) -> a c", a=1)).then_inc(bl_loaded, 16)
            for k in range(K):
                sp.wait_ge(table_lo, k + 1)
                sp.dma_start(gate_table[0][k * P:(k + 1) * P, :],
                             table_sb[:, k, :, :].rearrange("p a g -> p (a g)")).then_inc(table_stored, 16)
            sp.dma_start(rgcn_sb[:, :, :], rgcn_w.rearrange("r i o -> i r o")).then_inc(rgcn_loaded, 16)
            for buf, a in ((src_edges, src), (dst_edges, dst), (rel_edges, rel), (norm_edges, edge_w)):
                sp.dma_start(buf[:, :], a.rearrange("(p t) -> p t", p=P)).then_inc(edges_loaded, 16)
            for k in range(K):
                sp.wait_ge(table_lo, K + k + 1)
                sp.dma_start(gate_table[1][k * P:(k + 1) * P, :],
                             table_sb[:, k, :, :].rearrange("p a g -> p (a g)")).then_inc(table_stored, 16)
            for k in range(K):
                sp.wait_ge(msg_taken, k + 1)
                sp.dma_start(msg_table[k * P:(k + 1) * P, :], table2_sb[:, k, :]).then_inc(msg_stored, 16)
            for k in range(K):
                sp.wait_ge(result_ready, k + 1)
                sp.dma_start(out[k * P:(k + 1) * P, :], result[:, k, :]).then_inc(result_stored, 16)
            sp.wait_ge(result_stored, 16 * K)

        @block.gpsimd
        def _(pool):
            def hold(semaphore, value):
                pool.wait_ge(semaphore, value)
                pool.sem_inc(held, 1)

            def stage(j, indices, staged):
                pool.tensor_copy(index_now[:, j * K:(j + 1) * K], indices).then_inc(index_staged, 1)
                hold(index_staged, staged)

            pool.memset(ident[:, :], 0.0).then_inc(ident_ready, 1)
            pool.wait_ge(ident_ready, 1)
            pool.affine_select(out=ident[:, :], in_=ident[:, :], compare_op=ALU.not_equal, fill=1.0, base=0,
                               pattern=[[-1, P]], channel_multiplier=1).then_inc(ident_ready, 1)
            pool.iota(node_iota_i[:, :], pattern=[[1, N]], base=0, channel_multiplier=0).then_inc(iota_ready, 1)
            for h in range(2):
                pool.sem_inc(rows_free[h], UN)
            pool.sem_inc(msg_lo_ready, SLOTS)
            pool.wait_ge(index_ready, 1)

            for l in range(2):
                pool.wait_ge(table_stored, 16 * K * (l + 1))
                with pool.Fori(0, IT) as i:
                    for j in range(UN):
                        for h in range(2):
                            hold(rows_free[h], i * UN + (l * T + j + 1))
                        stage(j, src_steps[:, bass.ds(i * UN + j, 1), :].rearrange("p t k -> p (t k)"),
                              i * UN + (l * T + j + 1))
                        for s in range(j * K, (j + 1) * K):
                            pool.indirect_dma_start(
                                rows[:, s, :, :].rearrange("p a g -> p (a g)"), None, gate_table[l],
                                bass.IndirectOffsetOnAxis(index_now[:, s:s + 1], axis=0)).then_inc(rows_in[s], 16)

            pool.wait_ge(edge_ready, 2)
            pool.wait_ge(msg_stored, 16 * K)
            with pool.Fori(0, ET) as i:
                for j in range(UN):
                    hold(msg_lo_ready, i * SLOTS + (j + 1) * K)
                    stage(j, msg_index[:, bass.ds(i * SLOTS + j * K, K)], i * UN + (2 * T + j + 1))
                    for s in range(j * K, (j + 1) * K):
                        pool.indirect_dma_start(
                            edge_rows[:, s, :], None, msg_rows,
                            bass.IndirectOffsetOnAxis(index_now[:, s:s + 1], axis=0)).then_inc(rows_in[s], 16)

        @block.scalar
        def _(act):
            act.dma_start(wih_rows[0][:, :, :], wih[0].rearrange("(g p) c -> p g c", p=P)).then_inc(wih_loaded[0], 16)
            act.dma_start(bias_in[:, 0, 1, :], bhh[0].rearrange("(a g) -> a g", a=1)).then_inc(bias_loaded[0], 16)
            act.preload_act_table(ACT.Sigmoid)

            def take(group, dest):
                act.wait_ge(turned, group + 1)
                act.activation(dest, work[:, group % 4, :], ACT.Copy).then_inc(turned_act, 1)

            def table_parts(l):
                if l == 1:
                    act.wait_ge(table_stored, 16 * K)
                for k in range(K):
                    act.wait_ge(projected, l * K + k + 1)
                    act.activation(table_sb[:, k, 0, :], table_bank[l][k], ACT.Copy).then_inc(table_hi, 1)

            take(0, xT[:, :])
            table_parts(0)
            take(3, wihT[1][:, :])
            act.wait_ge(turned, 6)
            for a, scale in enumerate((1 / H_SCALE, 1.0) * 2):
                act.activation(linT[:, a, :], work[:, 1, a * C:(a + 1) * C], ACT.Copy,
                               scale=scale).then_inc(lin_ready, 1)

            for l in range(2):
                with act.Fori(0, IT) as i:
                    for j in range(UN):
                        def count(more=0):
                            return i * UN + (l * T + j + 1 + more)
                        for h in range(2):
                            act.wait_ge(gates0[h], count())
                            act.activation(act_if[:, h, :], gates[:, h, 0, :], ACT.Sigmoid,
                                           scale=1 / G_SCALE).then_inc(if_ready[h], 1)
                            act.wait_ge(gates1[h], count())
                            act.activation(act_g[:, h, :], gates[:, h, 1, 0:HN], ACT.Tanh,
                                           scale=1 / G_SCALE).then_inc(g_ready[h], 1)
                            other = 1 - h
                            act.wait_ge(h_full_ready[other], count(l) if other else count())
                            act.activation(h_hi[:, other, :], h_full[:, other, :], ACT.Copy
                                           ).then_inc(h_hi_ready[other], 1)
                            act.activation(act_o[:, h, :], gates[:, h, 1, HN:], ACT.Sigmoid,
                                           scale=1 / G_SCALE).then_inc(o_ready[h], 1)
                            act.wait_ge(c_ready[h], count())
                            act.activation(tanh_c[:, h, :], cell[:, h, :], ACT.Tanh).then_inc(tanh_ready[h], 1)
                if l == 0:
                    act.wait_ge(bl_loaded, 32)
                    act.wait_ge(sage_done, 1)
                    act.activation(h1T[:, :], work[:, 2, :], ACT.Relu, bias=bl1_col[:, :]).then_inc(h1T_ready, 1)
                    table_parts(1)

            act.preload_act_table(ACT.Sqrt)

            def norm_std(which):
                act.wait_ge(ln, which * (2 * K + 3) + 2 * K + 2)
                act.activation(std[:, :], var_eps[:, :], ACT.Sqrt).then_inc(ln_std, 1)

            norm_std(0)
            act.wait_ge(x2_turned, 1)
            act.activation(x2T[:, :], work[:, 0, :], ACT.Copy).then_inc(x2T_ready, 1)
            for k in range(0, K, 2):
                act.wait_ge(msg_projected, k + 1)
                if k >= 2:
                    act.wait_ge(msg_taken, k)
                act.activation(table2_sb[:, k, :], gate_bank[k][:, 0:NR * C], ACT.Copy).then_inc(msg_taken, 1)

            with act.Fori(0, ET) as i:
                for s in range(SLOTS):
                    act.wait_ge(rows_in[s], i * 16 + 16 * (2 * IT + 1))
                    act.wait_ge(msg_free, i * SLOTS + (s + 1))
                    act.activation(msg_hi[:, s, :], edge_rows[:, s, :], ACT.Copy,
                                   scale=norm_edges[:, bass.ds(i * SLOTS + s, 1)]).then_inc(msg_hi_ready, 1)

            act.wait_ge(agg_done, 1)
            act.activation(aggT[:, :], work[:, 1, :], ACT.Relu).then_inc(aggT_ready, 1)
            norm_std(1)

        @block.vector
        def _(dve):
            def take(group, dest):
                dve.wait_ge(turned, group + 1)
                dve.tensor_copy(dest, work[:, group % 4, :]).then_inc(turned_dve, 1)

            def split_whh(group, l):
                dve.wait_ge(turned, group + 1)
                dve.tensor_scalar(whh_hi[l][:, :], work[:, group % 4, :], W_SCALE, None,
                                  op0=ALU.mult).then_inc(whh_ready, 1)
                dve.wait_ge(whh_ready, 2 * l + 1)
                dve.scalar_tensor_tensor(whh_lo[l][:, :], work[:, group % 4, :], W_SCALE, whh_hi[l][:, :],
                                         op0=ALU.mult, op1=ALU.subtract).then_inc(whh_ready, 1)

            def table_parts(l):
                for k in range(K):
                    dve.wait_ge(table_hi, l * K + k + 1)
                    dve.tensor_tensor(table_sb[:, k, 1, :], table_bank[l][k], table_sb[:, k, 0, :],
                                      ALU.subtract).then_inc(table_lo, 1)

            def zero_state(l):
                dve.memset(cell[:, :, :], 0.0)
                dve.memset(h_full[:, 1, :], 0.0).then_inc(h_full_ready[1], 1)
                dve.memset(h_hi[:, 0, :], 0.0).then_inc(h_hi_ready[0], 1)
                dve.memset(h_lo[:, 0, :], 0.0).then_inc(h_lo_ready[0], 1)

            def bias_parts(l):
                dve.wait_ge(bias_loaded[l], 32)
                dve.tensor_tensor(bias_sum[:, l, :], bias_in[:, l, 0, :], bias_in[:, l, 1, :],
                                  ALU.add).then_inc(bias_ready, 1)
                dve.wait_ge(bias_ready, 3 * l + 1)
                dve.tensor_copy(bias_hi[:, l, :], bias_sum[:, l, :]).then_inc(bias_ready, 1)
                dve.wait_ge(bias_ready, 3 * l + 2)
                dve.tensor_tensor(bias_lo[:, l, :], bias_sum[:, l, :], bias_hi[:, l, :],
                                  ALU.subtract).then_inc(bias_ready, 1)

            dve.memset(zeros16[:, :], 0.0).then_inc(warm_ready, 1)
            dve.memset(ones16[:, :], 1.0)
            dve.memset(ones_row[:, :], 1.0)
            bias_parts(0)
            take(1, wihT[0][:, :])
            dve.wait_ge(ident_ready, 2)
            dve.tensor_scalar(ident_scaled[:, :], ident[:, :], G_SCALE, None, op0=ALU.mult).then_inc(ident16_ready, 1)
            dve.wait_ge(src_loaded, 16)
            dve.tensor_copy(src_steps[:, :, :].rearrange("p t k -> p k t"), src_by_node[:, :, :]).then_inc(index_ready, 1)
            zero_state(0)
            table_parts(0)
            split_whh(2, 0)
            split_whh(4, 1)
            bias_parts(1)
            dve.wait_ge(iota_ready, 1)
            dve.tensor_copy(node_iota[:, :], node_iota_i[:, :])
            dve.wait_ge(edges_loaded, 64)
            dve.tensor_copy(dst_f[:, :], dst_edges[:, :]).then_inc(edge_ready, 1)
            dve.scalar_tensor_tensor(msg_index[:, :], src_edges[:, :], float(NR), rel_edges[:, :],
                                     op0=ALU.mult, op1=ALU.add).then_inc(edge_ready, 1)

            for l in range(2):
                if l == 1:
                    zero_state(1)
                with dve.Fori(0, IT) as i:
                    for j in range(UN):
                        def count(more=0):
                            return i * UN + (l * T + j + 1 + more)
                        for h in range(2):
                            other = 1 - h
                            dve.wait_ge(if_ready[h], count())
                            dve.tensor_tensor(prod_fc[:, h, :], act_if[:, h, HN:], cell[:, h, :],
                                              ALU.mult).then_inc(fc_ready[h], 1)
                            dve.wait_ge(g_ready[h], count())
                            dve.tensor_tensor(prod_ig[:, h, :], act_if[:, h, 0:HN], act_g[:, h, :],
                                              ALU.mult).then_inc(ig_ready[h], 1)
                            dve.wait_ge(h_hi_ready[other], count() if other else count(l + 1))
                            dve.tensor_tensor(h_lo[:, other, :], h_full[:, other, :], h_hi[:, other, :],
                                              ALU.subtract).then_inc(h_lo_ready[other], 1)
                            dve.wait_ge(fc_ready[h], count())
                            dve.wait_ge(ig_ready[h], count())
                            dve.tensor_tensor(cell[:, h, :], prod_ig[:, h, :], prod_fc[:, h, :],
                                              ALU.add).then_inc(c_ready[h], 1)
                            dve.wait_ge(o_ready[h], count(1))
                            dve.wait_ge(tanh_ready[h], count())
                            dve.scalar_tensor_tensor(h_full[:, h, :], act_o[:, h, :], H_SCALE, tanh_c[:, h, :],
                                                     op0=ALU.mult, op1=ALU.mult).then_inc(h_full_ready[h], 1)
                if l == 0:
                    table_parts(1)

            steps = [0]

            def link(ins):
                steps[0] += 1
                ins.then_inc(ln, 1)

            def layer_norm(which, summand, residual, dest, ready):
                link(dve.tensor_tensor(y[:, :, :], summand, residual, ALU.add))
                dve.wait_ge(ln, steps[0])
                for k in range(K):
                    link(dve.bn_stats(stats[:, k, :], y[:, k, :]))
                for k in range(K):
                    dve.wait_ge(ln, steps[0] - K + 1)
                    link(dve.bn_aggr(mean_var[:, k, :], stats[:, k, :]))
                dve.wait_ge(ln, steps[0])
                link(dve.tensor_scalar(var_eps[:, :], mean_var[:, :, 1], EPS, None, op0=ALU.add))
                dve.wait_ge(ln_std, which + 1)
                link(dve.reciprocal(rstd[:, :], std[:, :]))
                dve.wait_ge(ln, steps[0])
                for k in range(K):
                    dve.tensor_scalar(dest[:, k, :], y[:, k, :], mean_var[:, k, 0:1], rstd[:, k:k + 1],
                                      op0=ALU.subtract, op1=ALU.mult).then_inc(ready, 1)

            dve.wait_ge(sage_done, 2)
            layer_norm(0, work[:, 3, :].rearrange("p (k c) -> p k c", k=K), x_nodes[:, :, :], x2, x2_ready)
            for k in range(1, K, 2):
                dve.wait_ge(msg_projected, k + 1)
                dve.wait_ge(msg_taken, k)
                dve.tensor_copy(table2_sb[:, k, :], gate_bank[k][:, 0:NR * C]).then_inc(msg_taken, 1)

            with dve.Fori(0, ET) as i:
                for s in range(SLOTS):
                    dve.wait_ge(msg_free, i * SLOTS + (s + 1))
                    dve.tensor_scalar(dst_onehot[:, s, :], node_iota[:, :], dst_f[:, bass.ds(i * SLOTS + s, 1)], None,
                                      op0=ALU.is_equal).then_inc(onehot_ready, 1)
                    dve.wait_ge(msg_hi_ready, i * SLOTS + (s + 1))
                    dve.scalar_tensor_tensor(msg_lo[:, s, :], edge_rows[:, s, :],
                                             norm_edges[:, bass.ds(i * SLOTS + s, 1)], msg_hi[:, s, :],
                                             op0=ALU.mult, op1=ALU.subtract
                                             ).then_inc(msg_lo_ready, 1)

            dve.wait_ge(agg_turned, 1)
            layer_norm(1, work[:, 2, :].rearrange("p (k c) -> p k c", k=K), x2[:, :, :], result, result_ready)

        @block.tensor
        def _(pe):
            def turn(group, blocks):
                for b, a in enumerate(blocks):
                    mm = pe.transpose(work[:, group % 4, b * P:(b + 1) * P], a, ident[:, :])
                mm.then_inc(turned, 1)

            def add_bias(l, k):
                pe.matmul(table_bank[l][k], ones16[:, :], bias_hi[:, l, :], start=True, stop=False,
                          skip_group_check=True)
                pe.matmul(table_bank[l][k], ones16[:, :], bias_lo[:, l, :], start=False, stop=False,
                          skip_group_check=True)

            def project(l, inT, k):
                pe.matmul(table_bank[l][k], inT[:, k * P:(k + 1) * P], wihT[l][:, :], start=False, stop=True,
                          skip_group_check=True).then_inc(projected, 1)

            def keep_warm(bank, n):
                for _ in range(n):
                    pe.matmul(bank, zeros16[:, 0:P], zeros16[:, :], start=True, stop=True)

            pe.wait_ge(warm_ready, 1)
            keep_warm(work[:, 3, :], WARM)
            pe.wait_ge(ident_ready, 2)
            pe.wait_ge(x_loaded, 16)
            turn(0, [x_nodes[:, k, :] for k in range(K)])
            pe.wait_ge(wih_loaded[0], 16)
            turn(1, [wih_rows[0][:, g, :] for g in range(4)])
            keep_warm(gate_bank[3], WARM)
            pe.wait_ge(bias_ready, 3)
            for k in range(K):
                add_bias(0, k)
            pe.wait_ge(turned_act, 1)
            pe.wait_ge(turned_dve, 1)
            for k in range(K):
                project(0, xT, k)
            pe.wait_ge(whh_loaded[0], 16)
            turn(2, [whh_rows[0][:, g, :] for g in range(4)])
            pe.wait_ge(wih_loaded[1], 16)
            turn(3, [wih_rows[1][:, g, :] for g in range(4)])
            pe.wait_ge(whh_loaded[1], 16)
            turn(4, [whh_rows[1][:, g, :] for g in range(4)])
            pe.wait_ge(lin_loaded, 64)
            turn(5, [lin_rows[:, g, :] for g in range(4)])
            pe.wait_ge(whh_ready, 4)
            pe.wait_ge(bias_ready, 6)
            pe.wait_ge(lin_ready, 4)
            for k in range(K - 1):
                add_bias(1, k)
            pe.matmul(work[:, 2, :], linT[:, 1, :], xT[:, :], start=True, stop=False, skip_group_check=True)
            for h in range(2):
                pe.sem_inc(o_ready[h], 1)
            pe.wait_ge(ident16_ready, 1)
            pe.wait_ge(table_lo, K)

            for l in range(2):
                with pe.Fori(0, IT) as i:
                    for j in range(UN):
                        def count(more=0):
                            return i * UN + (l * T + j + 1 + more)
                        for h in range(2):
                            for k in (2 * h, 2 * h + 1):
                                pe.wait_ge(rows_in[j * K + k], i * 16 + 16 * (l * IT + 1))
                            pe.wait_ge(o_ready[h], count())
                            for b in range(2):
                                for q, gate in enumerate(BANKS[b]):
                                    for k in range(2):
                                        for part in range(2):
                                            mm = pe.matmul(
                                                gates[:, h, b, q * HN + k * P:q * HN + (k + 1) * P],
                                                rows[:, j * K + 2 * h + k, part, gate * P:(gate + 1) * P],
                                                ident_scaled[:, :], start=(q == 0 and k == 0 and part == 0),
                                                stop=False, skip_group_check=True)
                            mm.then_inc(rows_free[h], 1)

                            def products(b, weights, state, last=False):
                                for q, gate in enumerate(BANKS[b]):
                                    for w in weights:
                                        mm = pe.matmul(gates[:, h, b, q * HN:(q + 1) * HN],
                                                       w[:, gate * P:(gate + 1) * P], state[:, h, :],
                                                       start=False, stop=last and q == 1, skip_group_check=True)
                                return mm
                            hi, lo = whh_hi[l], whh_lo[l]
                            pe.wait_ge(h_hi_ready[h], count() if h else count(l))
                            products(0, (hi, lo), h_hi)
                            pe.wait_ge(h_lo_ready[h], count() if h else count(l))
                            products(0, (hi,), h_lo, True).then_inc(gates0[h], 1)
                            products(1, (hi, lo), h_hi)
                            products(1, (hi,), h_lo, True).then_inc(gates1[h], 1)
                h_now = h_full[:, :, :].rearrange("p h n -> p (h n)")
                pe.wait_ge(o_ready[0], T * (l + 1) + 1)
                keep_warm(gate_bank[0], 2 * WARM)
                pe.wait_ge(h_full_ready[0], T * (l + 1))
                pe.wait_ge(h_full_ready[1], (T + 1) * (l + 1))
                if l == 0:
                    pe.matmul(work[:, 2, :], linT[:, 0, :], h_now, start=False, stop=True,
                              skip_group_check=True).then_inc(sage_done, 1)
                    keep_warm(gate_bank[0], WARM // 2)
                    pe.wait_ge(h1T_ready, 1)
                    for k in range(K - 1):
                        project(1, h1T, k)
                    add_bias(1, K - 1)
                    project(1, h1T, K - 1)
                    pe.wait_ge(bl_loaded, 32)
                    pe.wait_ge(table_lo, 2 * K)
                    for k in range(K):
                        o = work[:, 3, k * P:(k + 1) * P]
                        pe.matmul(o, h1T[:, k * P:(k + 1) * P], linT[:, 3, :], start=(k == 0), stop=False,
                                  skip_group_check=True)
                        pe.matmul(o, ones_row[:, :], bl2_row[:, :], start=False, stop=False,
                                  skip_group_check=True)
                else:
                    for k in range(K):
                        mm = pe.matmul(work[:, 3, k * P:(k + 1) * P], h_now[:, k * P:(k + 1) * P], linT[:, 2, :],
                                       start=False, stop=(k == K - 1), skip_group_check=True)
                    mm.then_inc(sage_done, 1)
                    keep_warm(gate_bank[0], 2 * WARM)

            for k in range(K):
                pe.wait_ge(x2_ready, k + 1)
                mm = pe.transpose(work[:, 0, k * P:(k + 1) * P], x2[:, k, :], ident[:, :])
            mm.then_inc(x2_turned, 1)
            pe.wait_ge(x2T_ready, 1)
            pe.wait_ge(rgcn_loaded, 16)
            for k in range(K):
                pe.matmul(gate_bank[k][:, 0:NR * C], x2T[:, k * P:(k + 1) * P],
                          rgcn_sb[:, :, :].rearrange("p r c -> p (r c)"), start=True, stop=True).then_inc(msg_projected, 1)

            pe.sem_inc(msg_free, SLOTS)
            pe.matmul(work[:, 1, :], zeros16[:, 0:P], zeros16[:, :], start=True, stop=False, skip_group_check=True)
            with pe.Fori(0, ET) as i:
                for s in range(SLOTS):
                    pe.wait_ge(msg_hi_ready, i * SLOTS + (s + 1))
                    pe.wait_ge(onehot_ready, i * SLOTS + (s + 1))
                    pe.matmul(work[:, 1, :], msg_hi[:, s, :], dst_onehot[:, s, :], start=False, stop=False,
                              skip_group_check=True)
                    pe.wait_ge(msg_lo_ready, i * SLOTS + (SLOTS + s + 1))
                    pe.matmul(work[:, 1, :], msg_lo[:, s, :], dst_onehot[:, s, :], start=False, stop=False,
                              skip_group_check=True).then_inc(msg_free, 1)
            pe.matmul(work[:, 1, :], zeros16[:, 0:P], zeros16[:, :], start=False, stop=True,
                      skip_group_check=True).then_inc(agg_done, 1)
            pe.wait_ge(aggT_ready, 1)
            for k in range(K):
                mm = pe.transpose(work[:, 2, k * P:(k + 1) * P], aggT[:, k * P:(k + 1) * P], ident[:, :])
            mm.then_inc(agg_turned, 1)


_LSTM = ["wih", "whh", "bih", "bhh", "wl", "bl", "wr"]
_INS = (["x", "src", "dst", "edge_type_3", "edge_weight"]
        + [f"L0_gnn_conv{l}_{w}" for l in (1, 2) for w in _LSTM] + ["L1_gnn_weight"])


def kernel(**inputs):
    import concourse.bacc as _bacc
    from concourse.bass_utils import run_bass_kernel_spmd as _run

    nc = _bacc.Bacc("TRN2", target_bir_lowering=False, num_devices=1)
    arrays, aps = {}, {}
    for name in _INS:
        a = np.ascontiguousarray(inputs[name])
        arrays[f"in_{name}"] = a
        aps[name] = nc.dram_tensor(f"in_{name}", a.shape, mybir.dt.from_np(a.dtype), kind="ExternalInput").ap()
    out = nc.dram_tensor("out", inputs["x"].shape, F32, kind="ExternalOutput").ap()
    both = {w: [aps[f"L0_gnn_conv{l}_{w}"] for l in (1, 2)] for w in _LSTM}
    build_program(nc, aps["x"], aps["src"], aps["dst"], aps["edge_type_3"], aps["edge_weight"],
                  both["wih"], both["whh"], both["bih"], both["bhh"], both["wl"], both["bl"], both["wr"],
                  aps["L1_gnn_weight"], out)
    r = _run(nc, [arrays], core_ids=[0])
    return r.results[0]["out"]
```

```python
from contextlib import ExitStack

import numpy as np

import concourse.bass as bass
from concourse import mybir

F32 = mybir.dt.float32
F16 = mybir.dt.float16
I32 = mybir.dt.int32
ACT = mybir.ActivationFunctionType
ALU = mybir.AluOpType

P = 128
H_SCALE = 2.0 ** 8
W_SCALE = 2.0 ** 7
G_SCALE = H_SCALE * W_SCALE
EPS = 1e-5
LO = 32
WARM = 6

GATE_I, GATE_F, GATE_G, GATE_O = range(4)
BANKS = ((GATE_I, GATE_F), (GATE_G, GATE_O))


def build_program(nc, x, src, dst, rel, edge_w, wih, whh, bih, bhh, wl, bl, wr, rgcn_w, out):
    N, C = x.shape
    E = src.shape[0]
    T = E // N
    NR = rgcn_w.shape[0]
    K = N // P
    G = 4 * C
    HN = N // 2
    UN = 4
    IT = (T - 1) // UN
    SLOTS = UN * K
    TILES = E // P
    BATCH = 4
    FIRST = BATCH
    order, seen = [], {"G": 0, "P": 0}
    for kind in "GGGP" * (2 * BATCH):
        order.append((kind == "P", seen[kind]))
        seen[kind] += 1
    NM, NG, NPE = len(order), seen["G"], seen["P"]
    ET = TILES // NM
    PT = ET * NPE + FIRST
    GT = ET * NG
    MS = NM // 2
    GB = NG // 2
    NB = NR * K
    assert C == P and (T - 1) % UN == 0 and TILES == PT + GT and N == G and MS + FIRST <= 2 * SLOTS

    gate_table = [nc.dram_tensor(f"gate_table{l}", (N, 2 * G), F16, kind="Internal").ap() for l in range(2)]
    msg_table = nc.dram_tensor("msg_table", (N, NR * C), F32, kind="Internal").ap()
    msg_rows = msg_table.rearrange("n (r c) -> (n r) c", c=C)
    code_table = nc.dram_tensor("code_table", (PT, P), F16, kind="Internal").ap()

    with ExitStack() as ctx:
        def sb(name, shape, dt):
            return ctx.enter_context(nc.sbuf_tensor(name, shape, dt))

        def sem(name):
            return ctx.enter_context(nc.semaphore(name))

        def pair(name):
            return [sem(f"{name}_{h}") for h in range(2)]

        gates = ctx.enter_context(nc.psum_tensor("gates", [P, 2, 2, 2 * HN], F32))
        work = ctx.enter_context(nc.psum_tensor("work", [P, 4, 512], F32))
        gate_bank = [gates[:, b // 2, b % 2, :] for b in range(4)]
        table_bank = [[gate_bank[2], gate_bank[3], work[:, 2, :], work[:, 3, :]],
                      [work[:, 0, :], work[:, 1, :], work[:, 3, :], gate_bank[2]]]
        sum_bank = [work[:, b, 0:HN] for b in (3, 2)]

        x_nodes = sb("x_nodes", [P, K, C], F32)
        wih_rows = [sb(f"wih_rows{l}", [P, 4, C], F32) for l in range(2)]
        whh_rows = [sb(f"whh_rows{l}", [P, 4, C], F32) for l in range(2)]
        lin_rows = sb("lin_rows", [P, 4, C], F32)
        bias_in = sb("bias_in", [1, 2, 2, G], F32)
        bias_sum = sb("bias_sum", [1, 2, G], F32)
        bias_parts = sb("bias_parts", [LO + 1, 2, G], F16)
        bl1_col = sb("bl1_col", [P, 1], F32)
        bl2_row = sb("bl2_row", [1, C], F32)
        rgcn_sb = sb("rgcn_sb", [P, NR, C], F32)
        src_by_node = sb("src_by_node", [P, K, T], I32)
        src_steps = sb("src_steps", [P, T, K], I32)
        src_edges = sb("src_edges", [P, GT], I32)
        rel_edges = sb("rel_edges", [P, GT], I32)
        msg_index = sb("msg_index", [P, GT], I32)
        src_tiles = sb("src_tiles", [PT, P], I32)
        rel_tiles = sb("rel_tiles", [PT, P], I32)
        code_tiles = sb("code_tiles", [PT, P], F16)
        dst_tiles = sb("dst_tiles", [PT, P], I32)
        dst_tiles_f = sb("dst_tiles_f", [PT, P], F32)
        norm_tiles = sb("norm_tiles", [PT, P], F32)
        dst_edges = sb("dst_edges", [P, GT], I32)
        norm_edges = sb("norm_edges", [P, TILES], F32)
        dst_f = sb("dst_f", [P, TILES], F32)
        index_now = sb("index_now", [P, NG], I32)

        ident = sb("ident", [P, P], F32)
        ident_scaled = sb("ident_scaled", [P, P], F16)
        ones_row = sb("ones_row", [1, P], F32)
        ones16 = sb("ones16", [LO + 1, P], F16)
        zeros16 = sb("zeros16", [P, 512], F16)
        node_iota_i = sb("node_iota_i", [P, N], I32)
        node_iota = sb("node_iota", [P, N], F16)
        block_iota_i = sb("block_iota_i", [P, NB], I32)
        block_iota = sb("block_iota", [P, NB], F32)

        xT = sb("xT", [P, N], F32)
        wihT = [sb(f"wihT{l}", [P, G], F32) for l in range(2)]
        whh_hi = [sb(f"whh_hi{l}", [P, G], F16) for l in range(2)]
        whh_lo = [sb(f"whh_lo{l}", [P, G], F16) for l in range(2)]
        linT = sb("linT", [P, 4, C], F32)

        src0_cols = sb("src0_cols", [P, K, P], F16)
        src0_row = sb("src0_row", [P, N], F16)
        src0_onehot = sb("src0_onehot", [P, K, N], F16)

        table_sb = sb("table_sb", [P, K, 2, G], F16)
        rows = sb("rows", [P, SLOTS, 2, G], F16)

        act_g = sb("act_g", [P, 2, HN], F32)
        act_if = sb("act_if", [P, 2, 2 * HN], F32)
        act_o = sb("act_o", [P, 2, HN], F32)
        tanh_c = sb("tanh_c", [P, 2, HN], F32)
        prod_ig = sb("prod_ig", [P, 2, HN], F32)
        prod_fc = sb("prod_fc", [P, 2, HN], F32)
        cell = sb("cell", [P, 2, HN], F32)
        h_full = sb("h_full", [P, 2, HN], F32)
        h_hi = sb("h_hi", [P, 2, HN], F16)
        h_lo = sb("h_lo", [P, 2, HN], F16)
        h1T = sb("h1T", [P, N], F32)

        y = sb("y", [P, K, C], F32)
        stats = sb("stats", [P, K, 6], F32)
        mean_var = sb("mean_var", [P, K, 2], F32)
        var_eps = sb("var_eps", [P, K], F32)
        std = sb("std", [P, K], F32)
        rstd = sb("rstd", [P, K], F32)
        x2 = sb("x2", [P, K, C], F32)
        x2T = sb("x2T", [P, N], F32)
        table2_sb = sb("table2_sb", [P, K, NR * C], F32)
        table2_hi = sb("table2_hi", [P, K, NR * C], F16)
        table2_lo = sb("table2_lo", [P, K, NR * C], F16)
        edge_rows = sb("edge_rows", [P, NG, C], F32)
        msg_hi = sb("msg_hi", [P, MS + FIRST, C], F16)
        msg_lo = sb("msg_lo", [P, MS + FIRST, C], F16)
        dst_onehot = [rows[:, s // 2, s % 2, :] for s in range(MS + FIRST)]
        code = sb("code", [P, (PT + BATCH) * P], F16)
        code_onehot = sb("code_onehot", [P, 2, NB, BATCH * P], F16)
        aggT = sb("aggT", [P, N], F32)
        result = sb("result", [P, K, C], F32)

        x_loaded = sem("x_loaded")
        wih_loaded = [sem(f"wih_loaded{l}") for l in range(2)]
        whh_loaded = [sem(f"whh_loaded{l}") for l in range(2)]
        bias_loaded = [sem(f"bias_loaded{l}") for l in range(2)]
        src_loaded = sem("src_loaded")
        lin_loaded = sem("lin_loaded")
        bl_loaded = sem("bl_loaded")
        rgcn_loaded = sem("rgcn_loaded")
        edges_loaded = sem("edges_loaded")
        tiles_turned = sem("tiles_turned")
        tiles_taken = sem("tiles_taken")
        code_computed = sem("code_computed")
        code_stored = sem("code_stored")
        code_loaded = sem("code_loaded")
        ident_ready = sem("ident_ready")
        ident16_ready = sem("ident16_ready")
        iota_ready = sem("iota_ready")
        index_ready = sem("index_ready")
        edge_ready = sem("edge_ready")
        bias_zeroed = sem("bias_zeroed")
        bias_ready = sem("bias_ready")
        turned = sem("turned")
        turned_act = sem("turned_act")
        turned_dve = sem("turned_dve")
        src0_spread = sem("src0_spread")
        src0_turned = sem("src0_turned")
        src0_row_ready = sem("src0_row_ready")
        src0_ready = sem("src0_ready")
        whh_ready = sem("whh_ready")
        lin_ready = sem("lin_ready")
        warm_ready = sem("warm_ready")
        projected = sem("projected")
        table_hi = sem("table_hi")
        table_lo = sem("table_lo")
        table_stored = sem("table_stored")
        rows_in = [sem(f"rows_in{s}") for s in range(SLOTS)]
        rows_free = pair("rows_free")
        index_staged = sem("index_staged")
        held = sem("held")
        gates0 = pair("gates0")
        gates1 = pair("gates1")
        if_ready = pair("if_ready")
        g_ready = pair("g_ready")
        o_ready = pair("o_ready")
        ig_ready = pair("ig_ready")
        c_ready = pair("c_ready")
        tanh_ready = pair("tanh_ready")
        h_hi_ready = pair("h_hi_ready")
        h_full_ready = pair("h_full_ready")
        h_lo_ready = pair("h_lo_ready")
        sage_done = sem("sage_done")
        h1T_ready = sem("h1T_ready")
        ln = sem("ln")
        ln_std = sem("ln_std")
        x2_ready = sem("x2_ready")
        x2_turned = sem("x2_turned")
        x2T_ready = sem("x2T_ready")
        msg_projected = sem("msg_projected")
        msg_taken = sem("msg_taken")
        msg_stored = sem("msg_stored")
        table2_hi_ready = sem("table2_hi_ready")
        table2_lo_ready = sem("table2_lo_ready")
        edge_rows_in = [sem(f"edge_rows_in{s}") for s in range(NG)]
        code_onehot_ready = sem("code_onehot_ready")
        pe_gathered = sem("pe_gathered")
        msg_free = sem("msg_free")
        msg_hi_ready = sem("msg_hi_ready")
        msg_lo_ready = sem("msg_lo_ready")
        onehot_ready = sem("onehot_ready")
        aggT_ready = sem("aggT_ready")
        agg_turned = sem("agg_turned")
        result_ready = sem("result_ready")
        result_stored = sem("result_stored")

        def edge_column(i, m):
            by_pe, n = order[m]
            return bass.ds(i * NPE + (FIRST + n) if by_pe else i * NG + (PT + n), 1)

        def unscaled(by_pe, n):
            return gate_bank[n % 4][:, 0:C] if by_pe else edge_rows[:, n, :]

        def store_half(engine, h):
            engine.wait_ge(result_ready, 2 * (h + 1))
            engine.dma_start(out[h * HN:(h + 1) * HN, :].rearrange("(k p) c -> p k c", p=P),
                             result[:, 2 * h:2 * (h + 1), :]).then_inc(result_stored, 16)

        block = ctx.enter_context(nc.Block())

        @block.sync
        def _(sp):
            def store_chunk(l, k):
                sp.wait_ge(table_lo, l * K + k + 1)
                sp.dma_start(gate_table[l][k * P:(k + 1) * P, :],
                             table_sb[:, k, :, :].rearrange("p a g -> p (a g)")).then_inc(table_stored, 16)

            sp.dma_start(x_nodes[:, :, :], x.rearrange("(k p) c -> p k c", p=P)).then_inc(x_loaded, 16)
            sp.dma_start(bias_in[:, 0, 0, :], bih[0].rearrange("(a g) -> a g", a=1)).then_inc(bias_loaded[0], 16)
            sp.dma_start(whh_rows[0][:, :, :], whh[0].rearrange("(g p) c -> p g c", p=P)).then_inc(whh_loaded[0], 16)
            sp.dma_start(src_by_node[:, :, :], src.rearrange("(k p t) -> p k t", p=P, k=K)).then_inc(src_loaded, 16)
            sp.dma_start(wih_rows[1][:, :, :], wih[1].rearrange("(g p) c -> p g c", p=P)).then_inc(wih_loaded[1], 16)
            sp.dma_start(whh_rows[1][:, :, :], whh[1].rearrange("(g p) c -> p g c", p=P)).then_inc(whh_loaded[1], 16)
            sp.dma_start(bias_in[:, 1, 0, :], bih[1].rearrange("(a g) -> a g", a=1)).then_inc(bias_loaded[1], 16)
            sp.dma_start(bias_in[:, 1, 1, :], bhh[1].rearrange("(a g) -> a g", a=1)).then_inc(bias_loaded[1], 16)
            for l in range(2):
                sp.dma_start(lin_rows[:, 2 * l, :], wl[l]).then_inc(lin_loaded, 16)
                sp.dma_start(lin_rows[:, 2 * l + 1, :], wr[l]).then_inc(lin_loaded, 16)
            sp.dma_start(bl1_col[:, :], bl[0].rearrange("(p a) -> p a", a=1)).then_inc(bl_loaded, 16)
            sp.dma_start(bl2_row[:, :], bl[1].rearrange("(a c) -> a c", a=1)).then_inc(bl_loaded, 16)
            for k in range(K):
                store_chunk(0, k)
            sp.dma_start(rgcn_sb[:, :, :], rgcn_w.rearrange("r i o -> i r o")).then_inc(rgcn_loaded, 16)
            for buf, a in ((src_tiles, src), (rel_tiles, rel), (dst_tiles, dst), (norm_tiles, edge_w)):
                sp.dma_start(buf[:, :], a[0:PT * P].rearrange("(t p) -> t p", p=P)).then_inc(edges_loaded, 16)
            for buf, a in ((src_edges, src), (rel_edges, rel)):
                sp.dma_start(buf[:, :], a[PT * P:].rearrange("(p t) -> p t", p=P)).then_inc(edges_loaded, 16)
            for buf, a in ((dst_edges[:, :], dst), (norm_edges[:, PT:], edge_w)):
                sp.dma_start(buf, a[PT * P:].rearrange("(p t) -> p t", p=P)).then_inc(edges_loaded, 16)
            sp.wait_ge(code_computed, 1)
            sp.dma_start(code_table, code_tiles[:, :]).then_inc(code_stored, 16)
            sp.wait_ge(code_stored, 16)
            sp.wait_ge(h_full_ready[0], T // 2)
            for t in range(0, PT, BATCH):
                sp.dma_start(code[:, t * P:(t + BATCH) * P],
                             code_table[t:t + BATCH, :].rearrange("t p -> (t p)").partition_broadcast(P)
                             ).then_inc(code_loaded, 16)
            for k in range(K):
                store_chunk(1, k)
            for k in range(K):
                sp.wait_ge(msg_taken, k + 1)
                sp.dma_start(msg_table[k * P:(k + 1) * P, :], table2_sb[:, k, :]).then_inc(msg_stored, 16)
            store_half(sp, 0)
            sp.wait_ge(result_stored, 32)

        @block.gpsimd
        def _(pool):
            def hold(semaphore, value):
                pool.wait_ge(semaphore, value)
                pool.sem_inc(held, 1)

            def stage(slots, indices, staged, table, stored):
                pool.tensor_copy(index_now[:, slots], indices).then_inc(index_staged, 1)
                pool.wait_ge(table, stored)
                hold(index_staged, staged)

            pool.memset(ident[:, :], 0.0).then_inc(ident_ready, 1)
            pool.wait_ge(ident_ready, 1)
            pool.affine_select(out=ident[:, :], in_=ident[:, :], compare_op=ALU.not_equal, fill=1.0, base=0,
                               pattern=[[-1, P]], channel_multiplier=1).then_inc(ident_ready, 1)
            pool.iota(node_iota_i[:, :], pattern=[[1, N]], base=0, channel_multiplier=0).then_inc(iota_ready, 1)
            pool.iota(block_iota_i[:, :], pattern=[[P, NB]], base=0, channel_multiplier=1).then_inc(iota_ready, 1)
            pool.wait_ge(iota_ready, 2)
            pool.tensor_copy(block_iota[:, :], block_iota_i[:, :]).then_inc(iota_ready, 1)
            for h in range(2):
                pool.sem_inc(rows_free[h], UN)
            pool.sem_inc(msg_lo_ready, NM)
            pool.wait_ge(index_ready, 1)

            for l in range(2):
                with pool.Fori(0, IT) as i:
                    for j in range(UN):
                        for h in range(2):
                            hold(rows_free[h], i * UN + (l * (T - 1) + j + 1))
                        stage(slice(j * K, (j + 1) * K),
                              src_steps[:, bass.ds(i * UN + (j + 1), 1), :].rearrange("p t k -> p (t k)"),
                              i * UN + (l * (T - 1) + j + 1), table_stored, 16 * K * (l + 1))
                        for s in range(j * K, (j + 1) * K):
                            pool.indirect_dma_start(
                                rows[:, s, :, :].rearrange("p a g -> p (a g)"), None, gate_table[l],
                                bass.IndirectOffsetOnAxis(index_now[:, s:s + 1], axis=0)).then_inc(rows_in[s], 16)

            pool.wait_ge(edge_ready, 3)
            for h in range(2):
                pool.wait_ge(rows_free[h], 2 * (T - 1) + UN)
            position = [m for m, (by_pe, _) in enumerate(order) if not by_pe]
            with pool.Fori(0, ET) as i:
                for j in range(2):
                    hold(msg_lo_ready, i * NM + (FIRST + position[(j + 1) * GB - 1] + 1))
                    stage(slice(j * GB, (j + 1) * GB), msg_index[:, bass.ds(i * NG + j * GB, GB)],
                          i * 2 + (2 * (T - 1) + j + 1), msg_stored, 16 * K)
                    for s in range(j * GB, (j + 1) * GB):
                        pool.indirect_dma_start(
                            edge_rows[:, s, :], None, msg_rows,
                            bass.IndirectOffsetOnAxis(index_now[:, s:s + 1], axis=0)).then_inc(edge_rows_in[s], 16)

        @block.scalar
        def _(act):
            act.dma_start(wih_rows[0][:, :, :], wih[0].rearrange("(g p) c -> p g c", p=P)).then_inc(wih_loaded[0], 16)
            act.dma_start(bias_in[:, 0, 1, :], bhh[0].rearrange("(a g) -> a g", a=1)).then_inc(bias_loaded[0], 16)
            act.preload_act_table(ACT.Sigmoid)

            def take(bank, groups, dest):
                act.wait_ge(turned, groups)
                act.activation(dest, work[:, bank, :], ACT.Copy).then_inc(turned_act, 1)

            def table_parts(l):
                if l == 1:
                    act.wait_ge(table_stored, 16 * K)
                for k in range(K):
                    act.wait_ge(projected, l * K + k + 1)
                    act.activation(table_sb[:, k, 0, :], table_bank[l][k], ACT.Copy).then_inc(table_hi, 1)
                    if l == 0 and k == 0:
                        act.wait_ge(src0_turned, 1)
                        act.activation(src0_row[:, :], gate_bank[0], ACT.Copy, scale=1 / G_SCALE
                                       ).then_inc(src0_row_ready, 1)

            take(0, 1, xT[:, :])
            table_parts(0)

            def tanh_of_cell(h, counted):
                act.wait_ge(c_ready[h], counted)
                act.activation(tanh_c[:, h, :], cell[:, h, :], ACT.Tanh).then_inc(tanh_ready[h], 1)

            def high_of_h(h, counted):
                act.wait_ge(h_full_ready[h], counted)
                act.activation(h_hi[:, h, :], h_full[:, h, :], ACT.Copy).then_inc(h_hi_ready[h], 1)

            def gates_i_f(h, counted, scale):
                act.wait_ge(gates0[h], counted)
                act.activation(act_if[:, h, :], gates[:, h, 0, :], ACT.Sigmoid, scale=scale).then_inc(if_ready[h], 1)

            def gate_g(h, counted, scale):
                act.wait_ge(gates1[h], counted)
                act.activation(act_g[:, h, :], gates[:, h, 1, 0:HN], ACT.Tanh, scale=scale).then_inc(g_ready[h], 1)

            def gate_o(h, scale):
                act.activation(act_o[:, h, :], gates[:, h, 1, HN:], ACT.Sigmoid, scale=scale).then_inc(o_ready[h], 1)

            for l in range(2):
                gates_i_f(0, l * T + 1, 1.0)
                gate_g(0, l * T + 1, 1.0)
                gate_o(0, 1.0)
                tanh_of_cell(0, l * T + 1)
                high_of_h(0, l * T + 1)
                if l == 0:
                    act.wait_ge(turned, 4)
                    for a, scale in enumerate((1 / H_SCALE, 1.0) * 2):
                        act.activation(linT[:, a, :], work[:, 1, a * C:(a + 1) * C], ACT.Copy,
                                       scale=scale).then_inc(lin_ready, 1)
                gates_i_f(1, l * T + 1, 1.0)
                gate_g(1, l * T + 1, 1.0)
                gate_o(1, 1.0)
                tanh_of_cell(1, l * T + 1)
                if l == 0:
                    take(3, 6, wihT[1][:, :])
                with act.Fori(0, IT) as i:
                    for j in range(UN):
                        now = i * UN + (l * T + j + 2)
                        high_of_h(1, i * UN + (l * T + j + 1))
                        gates_i_f(0, now, 1 / G_SCALE)
                        gate_g(0, now, 1 / G_SCALE)
                        gate_o(0, 1 / G_SCALE)
                        gates_i_f(1, now, 1 / G_SCALE)
                        gate_g(1, now, 1 / G_SCALE)
                        tanh_of_cell(0, now)
                        gate_o(1, 1 / G_SCALE)
                        high_of_h(0, now)
                        tanh_of_cell(1, now)

                def sage_relu(h):
                    act.wait_ge(sage_done, h + 1)
                    act.activation(h1T[:, h * HN:(h + 1) * HN], work[:, 2, h * HN:(h + 1) * HN], ACT.Relu,
                                   bias=bl1_col[:, :]).then_inc(h1T_ready, 1)

                if l == 0:
                    act.wait_ge(bl_loaded, 32)
                    sage_relu(0)
                    sage_relu(1)
                    table_parts(1)

            act.preload_act_table(ACT.Sqrt)

            def norm_std(which):
                act.wait_ge(ln, which * (2 * K + 4) + 2 * K + 3)
                act.activation(std[:, :], var_eps[:, :], ACT.Sqrt).then_inc(ln_std, 1)

            norm_std(0)
            for k in range(K):
                act.wait_ge(x2_turned, k + 1)
                act.activation(x2T[:, k * P:(k + 1) * P], work[:, k, 0:P], ACT.Copy).then_inc(x2T_ready, 1)
            for k in range(0, K, 2):
                act.wait_ge(msg_projected, k + 1)
                if k >= 2:
                    act.wait_ge(msg_taken, k)
                act.activation(table2_sb[:, k, :], gate_bank[k][:, 0:NR * C], ACT.Copy).then_inc(msg_taken, 1)
            for k in range(K):
                act.wait_ge(msg_taken, k + 1)
                act.activation(table2_hi[:, k, :], table2_sb[:, k, :], ACT.Copy).then_inc(table2_hi_ready, 1)

            def message_hi(slot, column, tile):
                act.activation(msg_hi[:, slot, :], unscaled(*tile), ACT.Copy,
                               scale=norm_edges[:, column]).then_inc(msg_hi_ready, 1)

            for n in range(FIRST):
                act.wait_ge(pe_gathered, n + 1)
                message_hi(MS + n, slice(n, n + 1), (True, n))
            with act.Fori(0, ET) as i:
                for m, (by_pe, n) in enumerate(order):
                    if by_pe:
                        act.wait_ge(pe_gathered, i * NPE + (FIRST + n + 1))
                    else:
                        act.wait_ge(edge_rows_in[n], i * 16 + 16)
                    act.wait_ge(msg_free, i * NM + (FIRST + m + 1))
                    message_hi(m % MS, edge_column(i, m), (by_pe, n))

            act.wait_ge(msg_free, TILES + MS)
            for h in range(2):
                act.activation(aggT[:, h * HN:(h + 1) * HN], work[:, 1, h * HN:(h + 1) * HN], ACT.Relu
                               ).then_inc(aggT_ready, 1)
            norm_std(1)
            store_half(act, 1)

        @block.vector
        def _(dve):
            def take(bank, groups, dest):
                dve.wait_ge(turned, groups)
                dve.tensor_copy(dest, work[:, bank, :]).then_inc(turned_dve, 1)

            def split_whh(bank, groups, l):
                dve.wait_ge(turned, groups)
                dve.tensor_scalar(whh_hi[l][:, :], work[:, bank, :], W_SCALE, None,
                                  op0=ALU.mult).then_inc(whh_ready, 1)
                dve.wait_ge(whh_ready, 2 * l + 1)
                dve.scalar_tensor_tensor(whh_lo[l][:, :], work[:, bank, :], W_SCALE, whh_hi[l][:, :],
                                         op0=ALU.mult, op1=ALU.subtract).then_inc(whh_ready, 1)

            def table_parts(l):
                for k in range(K):
                    dve.wait_ge(table_hi, l * K + k + 1)
                    dve.tensor_tensor(table_sb[:, k, 1, :], table_bank[l][k], table_sb[:, k, 0, :],
                                      ALU.subtract).then_inc(table_lo, 1)
                    if l == 0 and k < 2:
                        dve.wait_ge(src0_row_ready, 1)
                        dve.wait_ge(iota_ready, 3)
                        for b in (2 * k, 2 * k + 1):
                            dve.tensor_scalar(src0_onehot[:, b, :], src0_row[:, :], block_iota[:, b:b + 1], None,
                                              op0=ALU.is_equal).then_inc(src0_ready, 1)

            def split_bias(l, between=lambda: None):
                dve.wait_ge(bias_loaded[l], 32)
                dve.tensor_tensor(bias_sum[:, l, :], bias_in[:, l, 0, :], bias_in[:, l, 1, :],
                                  ALU.add).then_inc(bias_ready, 1)
                dve.wait_ge(bias_zeroed, 1)
                dve.wait_ge(bias_ready, 3 * l + 1)
                dve.tensor_copy(bias_parts[0:1, l, :], bias_sum[:, l, :]).then_inc(bias_ready, 1)
                between()
                dve.wait_ge(bias_ready, 3 * l + 2)
                dve.tensor_tensor(bias_parts[LO:LO + 1, l, :], bias_sum[:, l, :], bias_parts[0:1, l, :],
                                  ALU.subtract).then_inc(bias_ready, 1)

            dve.memset(zeros16[:, :], 0.0).then_inc(warm_ready, 1)
            dve.memset(ones16[:, :], 1.0)
            dve.memset(bias_parts[:, :, :], 0.0).then_inc(bias_zeroed, 1)
            dve.memset(ones_row[:, :], 1.0)
            split_bias(0, lambda: take(1, 2, wihT[0][:, :]))
            dve.wait_ge(ident_ready, 2)
            dve.tensor_scalar(ident_scaled[:, :], ident[:, :], G_SCALE, None, op0=ALU.mult).then_inc(ident16_ready, 1)
            dve.wait_ge(src_loaded, 16)
            dve.tensor_copy(src_steps[:, :, :].rearrange("p t k -> p k t"), src_by_node[:, :, :]).then_inc(index_ready, 1)
            dve.tensor_copy(src0_cols[:, :, :], src_by_node[:, :, 0:1].broadcast_to((P, K, P))).then_inc(src0_spread, 1)
            table_parts(0)

            def prepare_edges():
                dve.tensor_copy(node_iota[:, :], node_iota_i[:, :])
                dve.memset(code[:, PT * P:], 0.0)
                dve.wait_ge(edges_loaded, 128)
                dve.scalar_tensor_tensor(code_tiles[:, :], rel_tiles[:, :], float(N), src_tiles[:, :],
                                         op0=ALU.mult, op1=ALU.add).then_inc(code_computed, 1)
                dve.tensor_copy(dst_f[:, PT:], dst_edges[:, :]).then_inc(edge_ready, 1)
                dve.tensor_copy(dst_tiles_f[:, :], dst_tiles[:, :]).then_inc(edge_ready, 1)
                dve.scalar_tensor_tensor(msg_index[:, :], src_edges[:, :], float(NR), rel_edges[:, :],
                                         op0=ALU.mult, op1=ALU.add).then_inc(edge_ready, 1)

            def build_code(edges, buffer, b):
                dve.tensor_scalar(code_onehot[:, buffer, b, :], code[:, edges], block_iota[:, b:b + 1], None,
                                  op0=ALU.is_equal).then_inc(code_onehot_ready, 1)

            def new_h(h, counted):
                dve.wait_ge(tanh_ready[h], counted)
                dve.scalar_tensor_tensor(h_full[:, h, :], act_o[:, h, :], H_SCALE, tanh_c[:, h, :],
                                         op0=ALU.mult, op1=ALU.mult).then_inc(h_full_ready[h], 1)

            def low_of_h(h, counted):
                dve.wait_ge(h_hi_ready[h], counted)
                dve.tensor_tensor(h_lo[:, h, :], h_full[:, h, :], h_hi[:, h, :], ALU.subtract
                                  ).then_inc(h_lo_ready[h], 1)

            def first_cell(h):
                dve.wait_ge(g_ready[h], l * T + 1)
                dve.tensor_tensor(cell[:, h, :], act_if[:, h, 0:HN], act_g[:, h, :], ALU.mult).then_inc(c_ready[h], 1)

            def build_codes(blocks):
                if l == 1:
                    for b in blocks:
                        build_code(slice(0, BATCH * P), 0, b)

            for l in range(2):
                if l == 1:
                    dve.wait_ge(tiles_turned, 1)
                    dve.tensor_copy(dst_f[:, 0:PT], gate_bank[3][:, 0:PT]).then_inc(tiles_taken, 1)
                    dve.tensor_copy(norm_edges[:, 0:PT], gate_bank[3][:, PT:2 * PT]).then_inc(tiles_taken, 1)
                    dve.wait_ge(code_loaded, 16 * (PT // BATCH))
                build_codes(range(0, 6))
                first_cell(0)
                build_codes(range(6, 8))
                new_h(0, l * T + 1)
                if l == 0:
                    split_whh(2, 3, 0)
                    split_bias(1)
                low_of_h(0, l * T + 1)
                build_codes(range(8, NB))
                first_cell(1)
                new_h(1, l * T + 1)
                if l == 0:
                    split_whh(0, 5, 1)
                    prepare_edges()
                def products(h):
                    dve.wait_ge(if_ready[h], now)
                    dve.tensor_tensor(prod_fc[:, h, :], act_if[:, h, HN:], cell[:, h, :], ALU.mult)
                    dve.wait_ge(g_ready[h], now)
                    dve.tensor_tensor(prod_ig[:, h, :], act_if[:, h, 0:HN], act_g[:, h, :], ALU.mult
                                      ).then_inc(ig_ready[h], 1)

                def new_cell(h):
                    dve.wait_ge(ig_ready[h], step)
                    dve.tensor_tensor(cell[:, h, :], prod_ig[:, h, :], prod_fc[:, h, :], ALU.add
                                      ).then_inc(c_ready[h], 1)

                with dve.Fori(0, IT) as i:
                    for j in range(UN):
                        now = i * UN + (l * T + j + 2)
                        step = i * UN + (l * (T - 1) + j + 1)
                        low_of_h(1, step)
                        products(0)
                        new_cell(0)
                        products(1)
                        new_h(0, now)
                        new_cell(1)
                        low_of_h(0, now)
                        new_h(1, now)
                if l == 0:
                    table_parts(1)

            steps = [0]

            def link(ins):
                steps[0] += 1
                ins.then_inc(ln, 1)

            def layer_norm(which, summed, first, residual, dest, ready):
                for h in range(2):
                    chunks = (2 * h, 2 * h + 1)
                    dve.wait_ge(summed, first + h)
                    link(dve.tensor_tensor(y[:, 2 * h:2 * (h + 1), :], sum_bank[h].rearrange("p (k c) -> p k c", k=2),
                                           residual[:, 2 * h:2 * (h + 1), :], ALU.add))
                    dve.wait_ge(ln, steps[0])
                    for k in chunks:
                        link(dve.bn_stats(stats[:, k, :], y[:, k, :]))
                    for k in chunks:
                        dve.wait_ge(ln, steps[0] - 1)
                        link(dve.bn_aggr(mean_var[:, k, :], stats[:, k, :]))
                dve.wait_ge(ln, steps[0])
                link(dve.tensor_scalar(var_eps[:, :], mean_var[:, :, 1], EPS, None, op0=ALU.add))
                dve.wait_ge(ln_std, which + 1)
                link(dve.reciprocal(rstd[:, :], std[:, :]))
                dve.wait_ge(ln, steps[0])
                for k in range(K):
                    dve.tensor_scalar(dest[:, k, :], y[:, k, :], mean_var[:, k, 0:1], rstd[:, k:k + 1],
                                      op0=ALU.subtract, op1=ALU.mult).then_inc(ready, 1)

            layer_norm(0, sage_done, 3, x_nodes, x2, x2_ready)
            for k in range(1, K, 2):
                dve.wait_ge(msg_projected, k + 1)
                dve.wait_ge(msg_taken, k)
                dve.tensor_copy(table2_sb[:, k, :], gate_bank[k][:, 0:NR * C]).then_inc(msg_taken, 1)

            for k in range(K):
                dve.wait_ge(table2_hi_ready, k + 1)
                dve.tensor_tensor(table2_lo[:, k, :], table2_sb[:, k, :], table2_hi[:, k, :],
                                  ALU.subtract).then_inc(table2_lo_ready, 1)

            def onehot_of_destination(slot, column):
                dve.tensor_scalar(dst_onehot[slot], node_iota[:, :], dst_f[:, column], None,
                                  op0=ALU.is_equal).then_inc(onehot_ready, 1)

            def message_lo(slot, column, tile):
                dve.scalar_tensor_tensor(msg_lo[:, slot, :], unscaled(*tile), norm_edges[:, column],
                                         msg_hi[:, slot, :], op0=ALU.mult, op1=ALU.subtract
                                         ).then_inc(msg_lo_ready, 1)

            for n in range(FIRST):
                onehot_of_destination(MS + n, slice(n, n + 1))
            for n in range(FIRST):
                for b in range(n * NB // FIRST, (n + 1) * NB // FIRST):
                    build_code(slice(BATCH * P, 2 * BATCH * P), 1, b)
                dve.wait_ge(msg_hi_ready, n + 1)
                message_lo(MS + n, slice(n, n + 1), (True, n))
            with dve.Fori(0, ET) as i:
                for m, tile in enumerate(order):
                    dve.wait_ge(msg_free, i * NM + (FIRST + m + 1))
                    onehot_of_destination(m % MS, edge_column(i, m))
                    dve.wait_ge(msg_hi_ready, i * NM + (FIRST + m + 1))
                    message_lo(m % MS, edge_column(i, m), tile)
                    half, b = m // MS, m % MS
                    if b == 0:
                        dve.wait_ge(pe_gathered, i * NPE + (half + 1) * BATCH)
                    if b < NB:
                        build_code(bass.ds(i * (NPE * P) + (half + 2) * BATCH * P, BATCH * P), half, b)

            layer_norm(1, agg_turned, 1, x2, result, result_ready)

        @block.tensor
        def _(pe):
            def turn(bank, blocks):
                for b, a in enumerate(blocks):
                    mm = pe.transpose(work[:, bank, b * P:(b + 1) * P], a, ident[:, :])
                mm.then_inc(turned, 1)

            def add_bias(l, k, first=False, last=False):
                return pe.matmul(table_bank[l][k], ones16[:, :], bias_parts[:, l, :], start=first, stop=last,
                                 skip_group_check=True)

            def project(l, inT, k, first=False, last=False):
                return pe.matmul(table_bank[l][k], inT[:, k * P:(k + 1) * P], wihT[l][:, :], start=first, stop=last,
                                 skip_group_check=True)

            def keep_warm(bank, n):
                for _ in range(n):
                    pe.matmul(bank, zeros16[:, 0:P], zeros16[:, :], start=True, stop=True)

            pe.wait_ge(warm_ready, 1)
            keep_warm(work[:, 3, :], WARM)
            pe.wait_ge(ident_ready, 2)
            pe.wait_ge(x_loaded, 16)
            turn(0, [x_nodes[:, k, :] for k in range(K)])
            pe.wait_ge(wih_loaded[0], 16)
            turn(1, [wih_rows[0][:, g, :] for g in range(4)])
            keep_warm(gate_bank[3], 2)
            pe.wait_ge(turned_act, 1)
            pe.wait_ge(turned_dve, 1)
            def step0_gates(l, h, blocks):
                for k in blocks:
                    for b in range(2):
                        for q, gate in enumerate(BANKS[b]):
                            for part in range(2):
                                mm = pe.matmul(gates[:, h, b, q * HN:(q + 1) * HN],
                                               table_sb[:, k, part, gate * P:(gate + 1) * P],
                                               src0_onehot[:, k, h * HN:(h + 1) * HN],
                                               start=(k == 0 and q == 0 and part == 0),
                                               stop=(k == K - 1 and q == 1 and part == 1), skip_group_check=True)
                        if k == K - 1:
                            mm.then_inc((gates0, gates1)[b][h], 1)

            for k in range(K):
                project(0, xT, k, first=True)
                if k == 0:
                    pe.wait_ge(ident16_ready, 1)
                    pe.wait_ge(src0_spread, 1)
                    for a in range(K):
                        mm = pe.matmul(gate_bank[0][:, a * P:(a + 1) * P], src0_cols[:, a, :], ident_scaled[:, :],
                                       start=(a == 0), stop=(a == K - 1), skip_group_check=True)
                    mm.then_inc(src0_turned, 1)
                pe.wait_ge(bias_ready, 3)
                add_bias(0, k, last=True).then_inc(projected, 1)
            pe.wait_ge(src0_ready, K)
            for k in range(K):
                pe.wait_ge(table_lo, k + 1)
                step0_gates(0, 0, (k,))
            pe.wait_ge(whh_loaded[0], 16)
            turn(2, [whh_rows[0][:, g, :] for g in range(4)])
            pe.wait_ge(lin_loaded, 64)
            turn(1, [lin_rows[:, g, :] for g in range(4)])
            step0_gates(0, 1, range(K))
            pe.wait_ge(whh_loaded[1], 16)
            turn(0, [whh_rows[1][:, g, :] for g in range(4)])
            pe.wait_ge(wih_loaded[1], 16)
            turn(3, [wih_rows[1][:, g, :] for g in range(4)])
            pe.wait_ge(whh_ready, 2)
            pe.wait_ge(lin_ready, 4)
            pe.matmul(work[:, 2, :], linT[:, 1, :], xT[:, :], start=True, stop=False, skip_group_check=True)

            for l in range(2):
                hi, lo = whh_hi[l], whh_lo[l]

                def input_part(h, b):
                    for q, gate in enumerate(BANKS[b]):
                        for k in range(2):
                            for part in range(2):
                                mm = pe.matmul(gates[:, h, b, q * HN + k * P:q * HN + (k + 1) * P],
                                               rows[:, j * K + 2 * h + k, part, gate * P:(gate + 1) * P],
                                               ident_scaled[:, :], start=(q == 0 and k == 0 and part == 0),
                                               stop=False, skip_group_check=True)
                    return mm

                def products(h, b, weights, state, last=False):
                    for q, gate in enumerate(BANKS[b]):
                        for w in weights:
                            mm = pe.matmul(gates[:, h, b, q * HN:(q + 1) * HN], w[:, gate * P:(gate + 1) * P],
                                           state[:, h, :], start=False, stop=last and q == 1,
                                           skip_group_check=True)
                    return mm

                with pe.Fori(0, IT) as i:
                    for j in range(UN):
                        before = i * UN + (l * T + j + 1)
                        for h in range(2):
                            for k in (2 * h, 2 * h + 1):
                                pe.wait_ge(rows_in[j * K + k], i * 16 + 16 * (l * IT + 1))
                            pe.wait_ge(if_ready[h], before)
                            input_part(h, 0)
                            pe.wait_ge(o_ready[h], before)
                            input_part(h, 1).then_inc(rows_free[h], 1)
                        for h in range(2):
                            split = i * UN + (l * (T - 1) + j + 1) if h else before
                            pe.wait_ge(h_hi_ready[h], split)
                            products(h, 0, (hi, lo), h_hi)
                            pe.wait_ge(h_lo_ready[h], split)
                            products(h, 0, (hi,), h_lo, True).then_inc(gates0[h], 1)
                            products(h, 1, (hi, lo), h_hi)
                            products(h, 1, (hi,), h_lo, True).then_inc(gates1[h], 1)

                def sage_node_major(h):
                    pe.wait_ge(h_full_ready[h], T * (l + 1))
                    for k in range(2):
                        mm = pe.matmul(sum_bank[h][:, k * P:(k + 1) * P], h_full[:, h, k * P:(k + 1) * P],
                                       linT[:, 2, :], start=False, stop=(k == 1), skip_group_check=True)
                    mm.then_inc(sage_done, 1)

                def sage_turned(h):
                    pe.wait_ge(h_full_ready[h], T * (l + 1))
                    pe.matmul(work[:, 2, h * HN:(h + 1) * HN], linT[:, 0, :], h_full[:, h, :], start=False, stop=True,
                              skip_group_check=True).then_inc(sage_done, 1)

                if l == 0:
                    pe.wait_ge(whh_ready, 4)
                    pe.wait_ge(bias_ready, 6)
                    pe.wait_ge(turned_act, 2)
                    keep_warm(work[:, 0, :], 3)
                    for k in range(K - 1):
                        add_bias(1, k, first=True)
                    sage_turned(0)
                    pe.wait_ge(o_ready[1], T)
                    add_bias(1, K - 1, first=True)
                    pe.wait_ge(h1T_ready, 1)
                    project(1, h1T, 0, last=True).then_inc(projected, 1)
                    sage_turned(1)
                    project(1, h1T, 1, last=True).then_inc(projected, 1)
                    pe.wait_ge(h1T_ready, 2)
                    project(1, h1T, 2, last=True).then_inc(projected, 1)
                    project(1, h1T, 3, last=True).then_inc(projected, 1)
                    pe.wait_ge(edge_ready, 3)
                    pe.transpose(gate_bank[3][:, 0:PT], dst_tiles_f[:, :], ident[0:PT, 0:PT])
                    pe.transpose(gate_bank[3][:, PT:2 * PT], norm_tiles[:, :], ident[0:PT, 0:PT]
                                 ).then_inc(tiles_turned, 1)
                    for k in range(K):
                        pe.wait_ge(table_lo, K + k + 1)
                        step0_gates(1, 0, (k,))
                    pe.wait_ge(tiles_taken, 2)
                    step0_gates(1, 1, range(K))
                    pe.wait_ge(bl_loaded, 32)
                    for k in range(K):
                        o = sum_bank[k // 2][:, k % 2 * P:(k % 2 + 1) * P]
                        pe.matmul(o, h1T[:, k * P:(k + 1) * P], linT[:, 3, :], start=(k % 2 == 0), stop=False,
                                  skip_group_check=True)
                        pe.matmul(o, ones_row[:, :], bl2_row[:, :], start=False, stop=False,
                                  skip_group_check=True)
                else:
                    keep_warm(work[:, 0, :], WARM)
                    sage_node_major(0)
                    keep_warm(work[:, 0, :], 2)
                    sage_node_major(1)
                    keep_warm(work[:, 0, :], 10)

            for k in range(K):
                pe.wait_ge(x2_ready, k + 1)
                pe.transpose(work[:, k, 0:P], x2[:, k, :], ident[:, :]).then_inc(x2_turned, 1)
            pe.wait_ge(rgcn_loaded, 16)
            for k in range(K):
                pe.wait_ge(x2T_ready, k + 1)
                pe.matmul(gate_bank[k][:, 0:NR * C], x2T[:, k * P:(k + 1) * P],
                          rgcn_sb[:, :, :].rearrange("p r c -> p (r c)"), start=True, stop=True).then_inc(msg_projected, 1)

            pe.sem_inc(msg_free, MS)
            pe.matmul(work[:, 1, :], zeros16[:, 0:P], zeros16[:, :], start=True, stop=False, skip_group_check=True)
            keep_warm(work[:, 0, :], 2 * WARM)
            pe.wait_ge(table2_lo_ready, K)

            def gather(buffer, n):
                for b in range(NB):
                    r, k = divmod(b, K)
                    for part, table in enumerate((table2_hi, table2_lo)):
                        mm = pe.matmul(gate_bank[n % 4][:, 0:C],
                                       code_onehot[:, buffer, b, n % BATCH * P:(n % BATCH + 1) * P],
                                       table[:, k, r * C:(r + 1) * C], start=(b == 0 and part == 0),
                                       stop=(b == NB - 1 and part == 1))
                mm.then_inc(pe_gathered, 1)

            def add_message(slot, hi_count, lo_count):
                pe.wait_ge(onehot_ready, hi_count)
                pe.wait_ge(msg_hi_ready, hi_count)
                pe.matmul(work[:, 1, :], msg_hi[:, slot, :], dst_onehot[slot], start=False, stop=False,
                          skip_group_check=True)
                pe.wait_ge(msg_lo_ready, lo_count)
                pe.matmul(work[:, 1, :], msg_lo[:, slot, :], dst_onehot[slot], start=False, stop=False,
                          skip_group_check=True).then_inc(msg_free, 1)

            pe.wait_ge(code_onehot_ready, NB)
            for n in range(FIRST - 1):
                gather(0, n)
            for n in range(FIRST):
                add_message(MS + n, n + 1, NM + n + 1)
                if n == 0:
                    gather(0, FIRST - 1)
            with pe.Fori(0, ET) as i:
                for m in range(NM):
                    by_pe, n = order[(m + 3) % NM]
                    if by_pe:
                        batch = n // BATCH
                        pe.wait_ge(code_onehot_ready, i * (2 * NB) + (batch + 2) * NB)
                        gather(1 - batch, n)
                    add_message(m % MS, i * NM + (FIRST + m + 1), i * NM + (NM + FIRST + m + 1))
            for h in range(2):
                pe.wait_ge(aggT_ready, h + 1)
                for k in range(2):
                    mm = pe.transpose(sum_bank[h][:, k * P:(k + 1) * P], aggT[:, h * HN + k * P:h * HN + (k + 1) * P],
                                      ident[:, :])
                mm.then_inc(agg_turned, 1)


_LSTM = ["wih", "whh", "bih", "bhh", "wl", "bl", "wr"]
_INS = (["x", "src", "dst", "edge_type_3", "edge_weight"]
        + [f"L0_gnn_conv{l}_{w}" for l in (1, 2) for w in _LSTM] + ["L1_gnn_weight"])


def kernel(**inputs):
    import concourse.bacc as _bacc
    from concourse.bass_utils import run_bass_kernel_spmd as _run

    nc = _bacc.Bacc("TRN2", target_bir_lowering=False, num_devices=1)
    arrays, aps = {}, {}
    for name in _INS:
        a = np.ascontiguousarray(inputs[name])
        arrays[f"in_{name}"] = a
        aps[name] = nc.dram_tensor(f"in_{name}", a.shape, mybir.dt.from_np(a.dtype), kind="ExternalInput").ap()
    out = nc.dram_tensor("out", inputs["x"].shape, F32, kind="ExternalOutput").ap()
    both = {w: [aps[f"L0_gnn_conv{l}_{w}"] for l in (1, 2)] for w in _LSTM}
    build_program(nc, aps["x"], aps["src"], aps["dst"], aps["edge_type_3"], aps["edge_weight"],
                  both["wih"], both["whh"], both["bih"], both["bhh"], both["wl"], both["bl"], both["wr"],
                  aps["L1_gnn_weight"], out)
    r = _run(nc, [arrays], core_ids=[0])
    return r.results[0]["out"]
```
